# Optimizing a Trainium2 kernel written in Bass

```python
import numpy as np
import jax
import jax.numpy as jnp

def _softmax(x, axis=-1):
    return jax.nn.softmax(x, axis=axis)

def _gelu(x):
    return jax.nn.gelu(x, approximate=True)

def _silu(x):
    return jax.nn.silu(x)

def _sigmoid(x):
    return jax.nn.sigmoid(x)

def _layernorm(x, axis=-1, eps=1e-05):
    m = jnp.mean(x, axis=axis, keepdims=True)
    v = jnp.var(x, axis=axis, keepdims=True)
    return (x - m) / jnp.sqrt(v + eps)

def _scatter_add(tgt, idx, src, axis=0):
    return tgt.at[idx].add(src)

def _segment_sum(src, seg, n):
    return jax.ops.segment_sum(src, seg, n)
kernel_name = 'mk_adj_ffn_d2_adj_r2_410dcb'

def setup_inputs(seed: int=0):
    np.random.seed(seed)
    _w = jnp.asarray

    def _rec_inputs():
        import jax
        import jax.numpy as jnp
        _gk = jax.random.key(seed)
        x = -0.0005207 + 1.001 * jax.random.normal(jax.random.fold_in(_gk, 1), (4096, 128), jnp.float32)
        _a = jax.random.bernoulli(jax.random.fold_in(_gk, 2), 0.000976562, (4096, 4096))
        _a = jnp.logical_or(_a, jnp.swapaxes(_a, -1, -2))
        _a = jnp.logical_or(_a, jnp.eye(4096, dtype=bool))
        _af = _a.astype(jnp.float32)
        _af = _af * jax.random.uniform(jax.random.fold_in(_gk, 3), (4096, 4096), jnp.float32, 0.05, 1)
        adj = _af
        return (x, adj)
    x, adj = _rec_inputs()

    def _L0_gnn_setup():
        import jax, jax.numpy as jnp
        import numpy as np
        N = 4096
        F_IN = 128
        F_OUT = 128
        key = jax.random.key(seed)
        k_x, k_adj, k_kernel, k_bias, k_beta = jax.random.split(key, 5)
        x = jax.random.normal(k_x, (N, F_IN), dtype=jnp.float32)
        adj = jax.random.uniform(k_adj, (N, N), dtype=jnp.float32)
        limit = float(np.sqrt(6.0 / (F_IN + F_OUT)))
        kernel = jax.random.uniform(k_kernel, (F_IN, F_OUT), dtype=jnp.float32, minval=-limit, maxval=limit)
        bias = 0.01 * jax.random.normal(k_bias, (F_OUT,), dtype=jnp.float32)
        beta = 0.01 * jax.random.normal(k_beta, (N,), dtype=jnp.float32)
        return {'x': x, 'adj': adj, 'kernel': kernel, 'bias': bias, 'beta': beta}
    _L0_gnn_all = _L0_gnn_setup()
    _L0_gnn_in = {k: v for k, v in _L0_gnn_all.items() if k in ('kernel', 'bias', 'beta')}
    del _L0_gnn_all

    def _L0_ffn_setup():
        import jax, jax.numpy as jnp
        import numpy as np
        E = 8
        K = 2
        D = 128
        H = 256
        DOUT = 128
        EPS = 1e-05
        key = jax.random.key(seed)
        ks = jax.random.split(key, 9)
        s = 0.02
        return {'x': jax.random.normal(ks[0], (4, 4096, D), jnp.float32), 'gamma': 1.0 + 0.05 * jax.random.normal(ks[1], (D,), jnp.float32), 'beta': 0.05 * jax.random.normal(ks[2], (D,), jnp.float32), 'Wr': 0.01 * jax.random.normal(ks[3], (D, E), jnp.float32), 'br': jnp.zeros((E,), jnp.float32), 'W1': s * jax.random.normal(ks[4], (E, D, H), jnp.float32), 'b1': s * jax.random.normal(ks[5], (E, H), jnp.float32), 'W2': s * jax.random.normal(ks[6], (E, H, DOUT), jnp.float32), 'b2': s * jax.random.normal(ks[7], (E, DOUT), jnp.float32)}
    _L0_ffn_all = _L0_ffn_setup()
    _L0_ffn_in = {k: v for k, v in _L0_ffn_all.items() if k in ('gamma', 'beta', 'Wr', 'br', 'W1', 'b1', 'W2', 'b2')}
    del _L0_ffn_all

    def _L1_gnn_setup():
        import jax, jax.numpy as jnp
        import numpy as np
        N = 4096
        D = 128
        CUTOFF = 1.0
        MU = 1.0
        SIGMA = 0.5

        def sensitivity(r, mu, sigma):
            return jnp.exp(-(1.0 / r - 1.0 / mu) ** 2 / (2.0 * sigma * sigma))
        key = jax.random.key(seed)
        k_z, k_d, k_w = jax.random.split(key, 3)
        z = jax.random.normal(k_z, (N, D), dtype=jnp.float32)
        dist_matrix = jax.random.uniform(k_d, (N, N), dtype=jnp.float32) * 2.0 + 0.05
        W = jax.random.normal(k_w, (D, D), dtype=jnp.float32)
        B = jnp.zeros((D,), dtype=jnp.float32)
        return {'z': z, 'dist_matrix': dist_matrix, 'W': W, 'B': B}
    _L1_gnn_all = _L1_gnn_setup()
    _L1_gnn_in = {k: v for k, v in _L1_gnn_all.items() if k in ('W', 'B')}
    del _L1_gnn_all

    def _L1_ffn_setup():
        import jax, jax.numpy as jnp
        import numpy as np
        D_MODEL = 128
        EXPERT_DIM = 256
        NUM_EXPERTS = 8
        TOP_K = 2
        SEQ_LEN = 1024
        BATCH = 2
        key = jax.random.key(seed)
        ks = jax.random.split(key, 8)
        s = 0.02
        x = jax.random.normal(ks[0], (SEQ_LEN, BATCH, D_MODEL), dtype=jnp.float32)
        Wg = jax.random.normal(ks[1], (D_MODEL, NUM_EXPERTS), dtype=jnp.float32) * s
        bg = jax.random.normal(ks[2], (NUM_EXPERTS,), dtype=jnp.float32) * s
        bias = jnp.zeros((NUM_EXPERTS,), dtype=jnp.float32)
        W1 = jax.random.normal(ks[3], (NUM_EXPERTS, D_MODEL, EXPERT_DIM), dtype=jnp.float32) * s
        b1 = jax.random.normal(ks[4], (NUM_EXPERTS, EXPERT_DIM), dtype=jnp.float32) * s
        W2 = jax.random.normal(ks[5], (NUM_EXPERTS, EXPERT_DIM, D_MODEL), dtype=jnp.float32) * s
        b2 = jax.random.normal(ks[6], (NUM_EXPERTS, D_MODEL), dtype=jnp.float32) * s
        return {'x': x, 'Wg': Wg, 'bg': bg, 'bias': bias, 'W1': W1, 'b1': b1, 'W2': W2, 'b2': b2}
    _L1_ffn_all = _L1_ffn_setup()
    _L1_ffn_in = {k: v for k, v in _L1_ffn_all.items() if k in ('Wg', 'bg', 'bias', 'W1', 'b1', 'W2', 'b2')}
    del _L1_ffn_all
    return {'x': x, 'adj': adj, 'L0_gnn_kernel': _L0_gnn_in['kernel'], 'L0_gnn_bias': _L0_gnn_in['bias'], 'L0_gnn_beta': _L0_gnn_in['beta'], 'L0_ffn_gamma': _L0_ffn_in['gamma'], 'L0_ffn_beta': _L0_ffn_in['beta'], 'L0_ffn_Wr': _L0_ffn_in['Wr'], 'L0_ffn_br': _L0_ffn_in['br'], 'L0_ffn_W1': _L0_ffn_in['W1'], 'L0_ffn_b1': _L0_ffn_in['b1'], 'L0_ffn_W2': _L0_ffn_in['W2'], 'L0_ffn_b2': _L0_ffn_in['b2'], 'L1_gnn_W': _L1_gnn_in['W'], 'L1_gnn_B': _L1_gnn_in['B'], 'L1_ffn_Wg': _L1_ffn_in['Wg'], 'L1_ffn_bg': _L1_ffn_in['bg'], 'L1_ffn_bias': _L1_ffn_in['bias'], 'L1_ffn_W1': _L1_ffn_in['W1'], 'L1_ffn_b1': _L1_ffn_in['b1'], 'L1_ffn_W2': _L1_ffn_in['W2'], 'L1_ffn_b2': _L1_ffn_in['b2']}

def reference(x, adj, L0_gnn_kernel, L0_gnn_bias, L0_gnn_beta, L0_ffn_gamma, L0_ffn_beta, L0_ffn_Wr, L0_ffn_br, L0_ffn_W1, L0_ffn_b1, L0_ffn_W2, L0_ffn_b2, L1_gnn_W, L1_gnn_B, L1_ffn_Wg, L1_ffn_bg, L1_ffn_bias, L1_ffn_W1, L1_ffn_b1, L1_ffn_W2, L1_ffn_b2):
    import jax
    import jax.numpy as jnp

    def _L0_gnn_ref(x, adj, kernel, bias, beta):
        import jax, jax.numpy as jnp
        import numpy as np
        N = 4096
        F_IN = 128
        F_OUT = 128
        scale = jnp.reciprocal(jnp.sum(adj, axis=1) + beta)
        agg = adj @ x + beta[:, None] * x
        return scale[:, None] * agg @ kernel + bias

    def _L0_ffn_ref(x, gamma, beta, Wr, br, W1, b1, W2, b2):
        import jax, jax.numpy as jnp
        import numpy as np
        E = 8
        K = 2
        D = 128
        H = 256
        DOUT = 128
        EPS = 1e-05
        mu = jnp.mean(x, axis=-1, keepdims=True)
        var = jnp.mean(jnp.square(x - mu), axis=-1, keepdims=True)
        xn = (x - mu) * jax.lax.rsqrt(var + EPS) * gamma + beta
        logits = jnp.einsum('bsd,de->bse', xn, Wr) + br
        top_vals, top_idx = jax.lax.top_k(logits, K)
        w = jax.nn.softmax(top_vals, axis=-1)
        w_full = jnp.einsum('bsk,bske->bse', w, jax.nn.one_hot(top_idx, E, dtype=w.dtype))
        y = jnp.zeros(x.shape[:-1] + (DOUT,), x.dtype)
        for e in range(E):
            h = jax.nn.gelu(jnp.einsum('bsd,dh->bsh', xn, W1[e]) + b1[e], approximate=False)
            y_e = jnp.einsum('bsh,hd->bsd', h, W2[e]) + b2[e]
            y = y + y_e * w_full[..., e, None]
        return y

    def _L1_gnn_ref(z, dist_matrix, W, B):
        import jax, jax.numpy as jnp
        import numpy as np
        N = 4096
        D = 128
        CUTOFF = 1.0
        MU = 1.0
        SIGMA = 0.5

        def sensitivity(r, mu, sigma):
            return jnp.exp(-(1.0 / r - 1.0 / mu) ** 2 / (2.0 * sigma * sigma))
        msg = z @ W + B
        sens = sensitivity(dist_matrix, MU, SIGMA)
        weights = jnp.where(dist_matrix < CUTOFF, sens, 0.0)
        return weights @ msg

    def _L1_ffn_ref(x, Wg, bg, bias, W1, b1, W2, b2):
        import jax, jax.numpy as jnp
        import numpy as np
        D_MODEL = 128
        EXPERT_DIM = 256
        NUM_EXPERTS = 8
        TOP_K = 2
        SEQ_LEN = 1024
        BATCH = 2
        x_flat = x.reshape(-1, D_MODEL)
        gate_logits = x_flat @ Wg + bg + bias
        topk_vals, topk_idx = jax.lax.top_k(gate_logits, TOP_K)
        topk_w = jax.nn.softmax(topk_vals, axis=-1)
        combine = (jax.nn.one_hot(topk_idx, NUM_EXPERTS, dtype=x.dtype) * topk_w[..., None]).sum(axis=1)
        h = jax.nn.relu(jnp.einsum('td,edh->teh', x_flat, W1) + b1)
        y = jnp.einsum('teh,ehd->ted', h, W2) + b2
        out = jnp.einsum('ted,te->td', y, combine)
        return out.reshape(x.shape)
    x = x + _L0_gnn_ref(_layernorm(x, axis=-1), adj, L0_gnn_kernel, L0_gnn_bias, L0_gnn_beta)
    x = x + _L0_ffn_ref(_layernorm(x, axis=-1)[None], L0_ffn_gamma, L0_ffn_beta, L0_ffn_Wr, L0_ffn_br, L0_ffn_W1, L0_ffn_b1, L0_ffn_W2, L0_ffn_b2)[0]
    x = x + _L1_gnn_ref(_layernorm(x, axis=-1), adj, L1_gnn_W, L1_gnn_B)
    x = x + _L1_ffn_ref(_layernorm(x, axis=-1)[None], L1_ffn_Wg, L1_ffn_bg, L1_ffn_bias, L1_ffn_W1, L1_ffn_b1, L1_ffn_W2, L1_ffn_b2)[0]
    return x

_drawn_inputs = setup_inputs


def setup_inputs(seed=0):
    import zlib

    import numpy as np

    out = dict(_drawn_inputs(seed))
    spreads = {'L0_ffn_br': (0.0, 0.1), 'L1_gnn_B': (0.0, 0.412), 'L1_ffn_bias': (0.0, 0.8)}
    factors = {'L0_gnn_bias': 2.693,
     'L0_gnn_beta': 8.0,
     'L0_ffn_gamma': 8.0,
     'L0_ffn_beta': 8.0,
     'L0_ffn_Wr': 3.565,
     'L0_ffn_b1': 8.0,
     'L1_ffn_Wg': 8.0,
     'L1_ffn_bg': 22.095,
     'L1_ffn_W1': 8.0,
     'L1_ffn_b1': 41.12,
     'L1_ffn_W2': 8.0,
     'L1_ffn_b2': 64.0,
     'L0_ffn_b2': 2.728}
    for name, (base, spread) in spreads.items():
        noise = np.random.default_rng([zlib.crc32(name.encode()), seed]).standard_normal(out[name].shape)
        drawn = base * np.exp(spread * noise) if base else spread * noise
        out[name] = jnp.asarray(drawn.astype(out[name].dtype))
    for name, factor in factors.items():
        out[name] = (out[name] * factor).astype(out[name].dtype)
    return out
```

```python
import concourse.bass as bass
from concourse import mybir
from contextlib import ExitStack


def gnn_moe_two_layers(nc, x_t, adj_t, kern0, bias0, beta_t, gamma, beta_ln, wr, br, w1a, b1a, w2a, b2a,
                       wm, bm, wg, bg, gate_bias, w1b, b1b, w2b, b2b, out):
    F32, F32R, U32 = mybir.dt.float32, mybir.dt.float32r, mybir.dt.uint32
    ALU, ACT = mybir.AluOpType, mybir.ActivationFunctionType

    P = 128
    N = adj_t.shape[0]
    D = kern0.shape[0]
    E = wr.shape[1]
    H = w1a.shape[1] // E
    HC = H // P
    T = N // P
    BK = 512
    NB = N // BK
    K4 = BK // P
    EPS = 1e-5
    G = 6
    NG = 5
    S1 = 3
    S2 = 5
    assert D == P and T == G * NG + 2 and NB == 8 and HC == 2 and E == 8
    CUTOFF = 1.0
    TINY = 1e-18

    ctx = ExitStack()
    with ctx:
        def sb(name, shape, dt=F32):
            return ctx.enter_context(nc.sbuf_tensor(name, shape, dt))

        def sem(name):
            return ctx.enter_context(nc.semaphore(name))

        TB = N * 4
        ARENA = (nc.sbuf_base + 31) // 32 * 32
        sb("arena", [P, (1 + NG + S2 + 1) * N + 8])

        def at(name, offset, shape, dt=F32):
            return nc.alloc_sbuf_tensor_at(name, shape, dt, offset=offset)

        R_C = ARENA + TB
        R_R = R_C + NG * TB
        R_A = R_R + S2 * TB
        X = at("X", ARENA, [P, N])
        seed = at("seed", R_C + (NG - 1) * TB, [2 * E, E * P])
        C = at("C", R_C, [P, NG * N])
        ring = [at(f"ring{s}", R_R + s * TB, [P, N]) for s in range(S2)]
        colsum = at("colsum", R_A, [P, N])
        MSG = at("MSG", R_A, [P, N])
        BB = BK * 4
        AG = at("AG", R_R, [P, N])
        o = R_R + TB
        hid = [at(f"hid{s}", o + s * HC * BB, [P, HC, BK]) for s in range(2)]
        XTh = [at(f"XTh{s}", o + (4 + s) * BB, [P, BK], F32R) for s in range(2)]
        XTl = [at(f"XTl{s}", o + (6 + s) * BB, [P, BK], F32R) for s in range(2)]
        o = R_R + 2 * TB
        XL = at("XL", o, [P, BK])
        YS = at("YS", o + BB, [P, BK])
        AGS = at("AGS", o + 2 * BB, [P, BK])
        xT = at("xT", o + 3 * BB, [P, BK])
        wT = [at(f"wT{s}", o + (4 + s) * BB, [2 * E, BK], F32R) for s in range(2)]
        WBY = E * H * 4
        W1h, W1l, W2, W1raw = [], [], [], []
        for L, o in ((0, R_R + 3 * TB), (1, R_C)):
            W1h.append(at(f"W1h{L}", o, [P, E * H], F32R))
            W1l.append(at(f"W1l{L}", o + WBY, [P, E * H], F32R))
            W2.append(at(f"W2_{L}", o + 2 * WBY, [P, E * HC * D]))
            W1raw.append(at(f"W1raw{L}", o + 3 * WBY, [P, E * H]))

        sel = sb("sel", [2 * E, E * P], F32R)
        ident = sb("ident", [P, P])
        Kw = sb("Kw", [P, D])
        Wm = sb("Wm", [P, D])
        Bm = sb("Bm", [P, D])
        B0 = sb("B0", [P, D])
        Wrt = [sb("Wr", [P, E]), sb("Wg", [P, E])]
        brt = [sb("br_bc", [P, E]), sb("bg_bc", [P, E])]
        gb_bc = sb("gb_bc", [P, E])
        gam = sb("gam", [P, 1])
        bet = sb("bet", [P, 1])
        b1t = [sb("b1_0", [P, E * HC]), sb("b1_1", [P, E * HC])]
        b2r = [sb("b2r0", [2 * E, D]), sb("b2r1", [2 * E, D])]
        b2h = [sb("b2h0", [2 * E, D], F32R), sb("b2h1", [2 * E, D], F32R)]
        b2l = [sb("b2l0", [2 * E, D], F32R), sb("b2l1", [2 * E, D], F32R)]
        btile = sb("btile", [P, T])
        scl = sb("scl", [P, T])
        ones = sb("ones", [P, 1])
        scratch = sb("scratch", [P, 1])
        tiny = sb("tiny", [P, 1])
        minus2 = sb("minus2", [P, 1])
        nhalf = sb("nhalf", [P, 8])
        euler = sb("euler", [P, K4])
        iota8 = sb("iota8", [P, E])
        xs = [sb(f"xs{s}", [P, D]) for s in range(2)]
        st = sb("st", [P, 8, 6])
        mv = sb("mv", [P, T, 2])
        ve = sb("ve", [P, T])
        rs = sb("rs", [P, T])
        lg = sb("lg", [P, K4, E])
        mx = sb("mx", [P, K4, 8])
        ix = sb("ix", [P, K4, 8], U32)
        ixf = sb("ixf", [P, 2, K4])
        dm = sb("dm", [P, K4])
        ex = sb("ex", [P, K4])
        sm = sb("sm", [P, K4])
        wp = sb("wp", [P, 2, K4])
        oh = sb("oh", [P, 2, K4, E])
        wf = sb("wf", [P, K4, E])
        wh = sb("wh", [P, K4, E], F32R)
        wcat = sb("wcat", [P, K4, 2 * E])

        bank = ctx.enter_context(nc.psum_tensor("bank", [P, 8, BK], F32))
        HB = [bank[:, 2 * s:2 * s + 2, :] for s in range(2)]
        YB = bank[:, 4, :]
        GB = [bank[:, 5 + s, :] for s in range(2)]
        MB = bank[:, 7, :]

        x_in = [sem(f"x_in{c}") for c in range(4)]
        params_in = sem("params_in")
        w_in = [sem("w_in0"), sem("w_in1")]
        loaded1 = [sem(f"loaded1_{s}") for s in range(S1)]
        loaded2 = [sem(f"loaded2_{s}") for s in range(S2)]
        consts = sem("consts")
        smalls = sem("smalls")
        stats_done = sem("stats_done")
        aggr_done = sem("aggr_done")
        var_ready = sem("var_ready")
        rstd_ready = sem("rstd_ready")
        normed = sem("normed")
        split_done = sem("split_done")
        tile_ready = sem("tile_ready")
        summed = sem("summed")
        prod1 = sem("prod1")
        c_masked = sem("c_masked")
        c_log = sem("c_log")
        c_inverse = sem("c_inverse")
        c_square = sem("c_square")
        c_ready = sem("c_ready")
        biased = sem("biased")
        evac1 = sem("evac1")
        sums_ready = sem("sums_ready")
        scl_ready = sem("scl_ready")
        staged = sem("staged")
        m_ready = sem("m_ready")
        m_free = sem("m_free")
        xh_ready = sem("xh_ready")
        xt_ready = sem("xt_ready")
        route = sem("route")
        gap_ready = sem("gap_ready")
        exp_ready = sem("exp_ready")
        gates_ready = sem("gates_ready")
        hid_ready = sem("hid_ready")
        acted = sem("acted")
        gb_ready = sem("gb_ready")
        gated = sem("gated")
        w2_done = sem("w2_done")
        y_out = sem("y_out")
        masked = sem("masked")
        logged = sem("logged")
        inverse = sem("inverse")
        square = sem("square")
        f_ready = sem("f_ready")
        msg_staged = sem("msg_staged")
        prod2 = sem("prod2")
        evac2 = sem("evac2")
        stored = sem("stored")

        def tile(t):
            return bass.ds(t * P, P)

        def blk(b):
            return bass.ds(b * BK, BK)

        def pre_no(b, k, n_pre, n_end):
            return k if isinstance(b, int) and b == 0 else b * (n_pre + n_end) + (k - n_end)

        def end_no(b, k, n_pre, n_end):
            if isinstance(b, int) and b == NB - 1:
                return NB * (n_pre + n_end) - n_end + k
            return b * (n_pre + n_end) + (2 * n_pre + k)

        M_PRE, M_END = 4, (3, 1)
        N_PRE, N_END = (2, 1), (1, 0)
        M_ALL = NB * (M_PRE + M_END[0])
        N_ALL = NB * (N_PRE[0] + N_END[0])
        N_FIRST = 4
        ROUTE = 10

        def m_pre(L, b, k):
            return pre_no(b, k, M_PRE, M_END[L]) + L * M_ALL

        def m_end(L, b, k):
            return end_no(b, k, M_PRE, M_END[L]) + L * M_ALL

        def n_pre(L, b, k):
            return pre_no(b, k, N_PRE[L], N_END[L]) + L * N_ALL

        def n_end(L, b):
            return end_no(b, 0, N_PRE[L], N_END[L]) + L * N_ALL

        def expert_no(L, b, e):
            return b * E + (L * NB * E + e)

        def blocks(eng, body):
            body(0, 0)
            with eng.Fori(0, (NB - 2) // 2) as g:
                body(g * 2 + 1, 1)
                body(g * 2 + 2, 0)
            body(NB - 1, 1)

        def first(b):
            return isinstance(b, int) and b == 0

        def last(b):
            return isinstance(b, int) and b == NB - 1

        params = [(Kw[:, :], kern0), (Wm[:, :], wm), (Bm[:, :], bm.partition_broadcast(P)),
                  (B0[:, :], bias0.partition_broadcast(P)), (Wrt[0][:, :], wr), (Wrt[1][:, :], wg),
                  (brt[0][:, :], br.partition_broadcast(P)), (brt[1][:, :], bg.partition_broadcast(P)),
                  (gb_bc[:, :], gate_bias.partition_broadcast(P)), (gam[:, :], gamma), (bet[:, :], beta_ln),
                  (b1t[0][:, :], b1a), (b1t[1][:, :], b1b), (btile[:, :], beta_t)]
        for L, b2 in ((0, b2a), (1, b2b)):
            params += [(b2r[L][0:E, :], b2), (b2r[L][E:2 * E, :], b2)]
        PARAMS = len(params)

        block = ctx.enter_context(nc.Block())

        @block.sync
        def _(sp):
            for c in range(4):
                sp.dma_start(X[:, c * 8 * P:(c + 1) * 8 * P], x_t[:, c * 8 * P:(c + 1) * 8 * P]).then_inc(x_in[c], 16)

            def load1(t, s):
                sp.wait_ge(prod1, t + 1)
                sp.wait_ge(summed, t + 1)
                sp.dma_start(ring[s][:, :], adj_t[tile(t), :]).then_inc(loaded1[s], 16)

            load1(0, 0)
            sp.dma_start(W1raw[0][:, :], w1a).then_inc(w_in[0], 16)
            sp.dma_start(W2[0][:, :], w2a).then_inc(w_in[0], 16)
            with sp.Fori(0, NG) as g:
                for k in range(G):
                    load1(g * G + (1 + k), (1 + k) % S1)
            load1(T - 1, (T - 1) % S1)

            def load2(t, s):
                sp.dma_start(ring[s][:, :], adj_t[tile(t), :]).then_inc(loaded2[s], 16)

            sp.wait_ge(m_free, M_ALL)
            for k in range(1, G):
                load2(1 + k, k - 1)
            with sp.Fori(1, NG) as g:
                for k in range(1, G):
                    sp.wait_ge(prod2, g * G + (k - G + 3))
                    load2(g * G + (1 + k), k - 1)
            sp.dma_start(W1raw[1][:, :], w1b).then_inc(w_in[1], 16)
            sp.dma_start(W2[1][:, :], w2b).then_inc(w_in[1], 16)
            for s, t in ((0, 0), (1, T - 1)):
                sp.wait_ge(prod2, (NG - 1) * G + (s + 1) + 3)
                load2(t, s)

            def store(b):
                sp.wait_ge(m_free, m_end(1, b, 0) + 1)
                sp.dma_start(out[:, blk(b)], X[:, blk(b)]).then_inc(stored, 16)

            with sp.Fori(0, NB - 1) as b:
                store(b)
            store(NB - 1)
            sp.wait_ge(stored, 16 * NB)

        @block.gpsimd
        def _(pool):
            pool.memset(ident[:, :], 0.0).then_inc(consts, 1)
            pool.memset(seed[:, :], 0.0).then_inc(consts, 1)
            pool.memset(ones[:, :], 1.0).then_inc(consts, 1)
            pool.memset(tiny[:, :], TINY).then_inc(consts, 1)
            pool.memset(minus2[:, :], -2.0).then_inc(consts, 1)
            pool.memset(nhalf[:, :], -0.5).then_inc(consts, 1)
            pool.memset(euler[:, :], 2.718281828459045).then_inc(consts, 1)
            pool.iota(iota8[:, :], [[1, E]], base=0, channel_multiplier=0,
                      allow_small_or_imprecise_dtypes=True).then_inc(consts, 1)
            pool.wait_ge(consts, 8)
            pool.affine_select(out=ident[:, :], in_=ident[:, :], compare_op=ALU.not_equal, fill=1.0, base=0,
                               pattern=[[-1, P]], channel_multiplier=1).then_inc(consts, 1)
            v = seed[:, :].rearrange("p (e q) -> p e q", q=P)
            for r in range(2):
                if r:
                    pool.wait_ge(consts, 10)
                pool.affine_select(out=v, in_=v, compare_op=ALU.not_equal, fill=1.0, base=-E * r,
                                   pattern=[[-1, E], [0, P]], channel_multiplier=1).then_inc(consts, 1)

            for c in range(N_FIRST):
                pool.wait_ge(var_ready, c + 1)
                pool.tensor_tensor(rs[:, 8 * c:8 * c + 8], ve[:, 8 * c:8 * c + 8], nhalf[:, :],
                                   ALU.pow).then_inc(rstd_ready, 1)
            pool.wait_ge(params_in, PARAMS * 16)
            for c in range(4):
                pool.wait_ge(tile_ready, 8 * c + 8)
                v = X[:, c * 8 * P:(c + 1) * 8 * P].rearrange("p (t d) -> p t d", d=D)
                pool.tensor_tensor(v, v, B0[:, :].unsqueeze(1).to_broadcast([P, 8, D]), ALU.add).then_inc(biased, 1)

            def power(n):
                pool.wait_ge(var_ready, n + (N_FIRST + 1))
                pool.tensor_tensor(rs[:, 0:K4], ve[:, 0:K4], nhalf[:, 0:K4], ALU.pow).then_inc(rstd_ready, 1)

            def pre(L, b):
                if not first(b):
                    pool.wait_ge(m_ready, m_pre(L, b - 1, 0) + 1)
                pool.tensor_copy(AGS[:, :], AG[:, blk(b)]).then_inc(staged, 1)
                for k in range(N_PRE[L]):
                    power(n_pre(L, b, k))
                pool.wait_ge(gap_ready, b + (NB * L + 1))
                pool.tensor_tensor(ex[:, :], euler[:, :], dm[:, :], ALU.pow).then_inc(exp_ready, 1)

            def end(L, b):
                for _ in range(N_END[L]):
                    power(n_end(L, b))

            def experts(L):
                pre(L, 0)
                pre(L, 1)
                end(L, 0)
                pre(L, 2)
                with pool.Fori(2, NB - 1) as b:
                    end(L, b - 1)
                    pre(L, b + 1)
                end(L, NB - 2)
                end(L, NB - 1)

            pool.wait_ge(evac1, NB)
            experts(0)

            def message(k, t, s):
                pool.wait_ge(prod2, k + 1)
                pool.tensor_copy(xs[s][:, :], MSG[:, tile(t)]).then_inc(msg_staged, 1)

            pool.wait_ge(m_free, M_ALL)
            with pool.Fori(0, NG) as g:
                for k in range(G):
                    message(g * G + k, g * G + (1 + k), k % 2)
            message(T - 2, 0, 0)
            message(T - 1, T - 1, 1)
            pool.wait_ge(evac2, NB)
            experts(1)

        @block.vector
        def _(dve):
            def settle():
                nc.vector.memset(scratch[:, :], 0.0)

            def norm_stats(n, src):
                settle()
                for k in range(K4):
                    ins = nc.vector.bn_stats(st[:, k, :], src(k))
                ins.then_inc(stats_done, 1)
                dve.wait_ge(stats_done, n + (N_FIRST + 1))
                settle()
                for k in range(K4):
                    ins = nc.vector.bn_aggr(mv[:, k, :], st[:, k, :])
                ins.then_inc(aggr_done, 1)
                dve.wait_ge(aggr_done, n + (N_FIRST + 1))
                nc.vector.tensor_scalar(ve[:, 0:K4], mv[:, 0:K4, 1], EPS, None, ALU.add).then_inc(var_ready, 1)

            def normalise(n, src):
                dve.wait_ge(rstd_ready, n + (N_FIRST + 1))
                for k in range(K4):
                    ins = nc.vector.tensor_scalar(XL[:, k * P:(k + 1) * P], src(k), mv[:, k, 0:1], rs[:, k:k + 1],
                                                  ALU.subtract, ALU.mult)
                ins.then_inc(normed, 1)

            def X_rows(b):
                return lambda k: X[:, tile(b * K4 + k)]

            def XL_rows(k):
                return XL[:, k * P:(k + 1) * P]

            dve.sem_inc(summed, S1)
            dve.sem_inc(gated, 2)
            nc.vector.memset(colsum[:, :], 0.0).then_inc(smalls, 1)
            for c in range(4):
                dve.wait_ge(x_in[c], 16)
                for k in range(8):
                    t = 8 * c + k
                    ins = nc.vector.bn_stats(st[:, k, :], X[:, t * P:(t + 1) * P])
                ins.then_inc(stats_done, 1)
                dve.wait_ge(stats_done, c + 1)
                for k in range(8):
                    ins = nc.vector.bn_aggr(mv[:, 8 * c + k, :], st[:, k, :])
                ins.then_inc(aggr_done, 1)
                dve.wait_ge(aggr_done, c + 1)
                nc.vector.tensor_scalar(ve[:, 8 * c:8 * c + 8], mv[:, 8 * c:8 * c + 8, 1], EPS, None,
                                        ALU.add).then_inc(var_ready, 1)
            dve.wait_ge(params_in, PARAMS * 16)
            for L in range(2):
                nc.vector.tensor_copy(b2h[L][:, :], b2r[L][:, :]).then_inc(smalls, 1)
            nc.vector.tensor_tensor(brt[1][:, :], brt[1][:, :], gb_bc[:, :], ALU.add).then_inc(smalls, 1)
            dve.wait_ge(smalls, 4)
            for L in range(2):
                nc.vector.tensor_tensor(b2l[L][:, :], b2r[L][:, :], b2h[L][:, :].bitcast(F32),
                                        ALU.subtract).then_inc(smalls, 1)
            dve.wait_ge(consts, 11)
            nc.vector.tensor_copy(sel[:, :], seed[:, :]).then_inc(smalls, 1)

            dve.wait_ge(rstd_ready, N_FIRST)

            def graph1_tile(t, s, xslot, arrivals, cached=None):
                dve.wait_ge(loaded1[s], arrivals * 16)
                if cached is not None:
                    nc.vector.scalar_tensor_tensor(C[:, bass.ds(cached * N, N)], ring[s][:, :], CUTOFF, ring[s][:, :],
                                                   ALU.is_lt, ALU.mult).then_inc(c_masked, 1)
                dve.wait_ge(prod1, t + 2)
                nc.vector.tensor_scalar(xs[xslot][:, :], X[:, tile(t)], mv[:, bass.ds(t, 1), 0], rs[:, bass.ds(t, 1)],
                                        ALU.subtract, ALU.mult)
                if cached is not None:
                    dve.wait_ge(c_masked, cached + 1)
                nc.vector.scalar_tensor_tensor(ring[s][:, tile(t)], ident[:, :], btile[:, bass.ds(t, 1)],
                                               ring[s][:, tile(t)], ALU.mult, ALU.add).then_inc(tile_ready, 1)
                dve.wait_ge(tile_ready, t + 1)
                dve.wait_ge(summed, t + S1)
                nc.vector.tensor_tensor(colsum[:, :], colsum[:, :], ring[s][:, :], ALU.add).then_inc(summed, 1)

            def square_cached(g):
                dve.wait_ge(c_inverse, g + 1)
                v = C[:, bass.ds(g * N, N)]
                nc.vector.scalar_tensor_tensor(v, v, 2.0, v, ALU.subtract, ALU.mult).then_inc(c_square, 1)

            def split_weights(L):
                dve.wait_ge(w_in[L], 32)
                nc.vector.tensor_copy(W1h[L][:, :], W1raw[L][:, :]).then_inc(split_done, 1)
                dve.wait_ge(split_done, 2 * L + 1)
                nc.vector.tensor_tensor(W1l[L][:, :], W1raw[L][:, :], W1h[L][:, :].bitcast(F32),
                                        ALU.subtract).then_inc(split_done, 1)

            graph1_tile(0, 0, 0, 1)
            split_weights(0)
            with dve.Fori(0, NG) as g:
                for k in range(G):
                    t = 1 + k
                    graph1_tile(g * G + t, t % S1, t % 2, g * 2 + (t // S1 + 1), g if k == 0 else None)
                    if k == 3:
                        square_cached(g)
            graph1_tile(T - 1, (T - 1) % S1, (T - 1) % 2, (T - 1) // S1 + 1)
            dve.wait_ge(prod1, T + S1)
            for b in range(4, 8):
                nc.vector.tensor_copy(AG[:, b * BK:(b + 1) * BK], bank[:, b, :]).then_inc(evac1, 1)
            dve.wait_ge(sums_ready, 1)
            nc.vector.reciprocal(scl[:, :], MB[:, 0:T]).then_inc(scl_ready, 1)
            dve.wait_ge(scl_ready, 1)
            dve.wait_ge(biased, 4)

            def gate_hidden(L, b, e):
                n = expert_no(L, b, e)
                dve.wait_ge(acted, n * 2 + 6)
                dve.wait_ge(gb_ready, n + 1)
                s = e % 2
                nc.vector.tensor_tensor(hid[s][:, :, :], hid[s][:, :, :],
                                        GB[s].unsqueeze(1).to_broadcast([P, HC, BK]), ALU.mult).then_inc(gated, 1)

            def add_graph(L, b):
                u = m_pre(L, b, 0)
                dve.wait_ge(m_ready, u + 1)
                if L == 0:
                    for k in range(K4):
                        t = b * K4 + k
                        ins = nc.vector.scalar_tensor_tensor(X[:, tile(t)], MB[:, k * P:(k + 1) * P],
                                                             scl[:, bass.ds(t, 1)], X[:, tile(t)], ALU.mult, ALU.add)
                else:
                    ins = nc.vector.tensor_tensor(X[:, blk(b)], MB, X[:, blk(b)], ALU.add)
                ins.then_inc(m_free, 1)
                dve.wait_ge(m_free, u + 1)
                norm_stats(n_pre(L, b, 0), X_rows(b))

            def first_norm(L, b):
                n = n_pre(L, b, 0)
                normalise(n, X_rows(b))
                if L == 0:
                    dve.wait_ge(normed, n + 1)
                    norm_stats(n_pre(L, b, 1), XL_rows)

            def second_norm(L, b):
                normalise(n_pre(L, b, 1), XL_rows)

            def low_part(L, b, par):
                dve.wait_ge(xh_ready, b + (NB * L + 1))
                nc.vector.tensor_tensor(XTl[par][:, :], xT[:, :], XTh[par][:, :].bitcast(F32),
                                        ALU.subtract).then_inc(xt_ready, 1)

            def route_first(L, b):
                u = m_pre(L, b, 2)
                r = b * ROUTE + NB * L * ROUTE
                dve.wait_ge(m_ready, u + 1)
                nc.vector.tensor_tensor(lg[:, :, :], MB[:, 0:K4 * E].rearrange("p (k e) -> p k e", e=E),
                                        brt[L][:, :].unsqueeze(1).to_broadcast([P, K4, E]), ALU.add).then_inc(m_free, 1)
                dve.wait_ge(m_free, u + 1)
                settle()
                for k in range(K4):
                    ins = nc.vector.max(mx[:, k, :], lg[:, k, :])
                ins.then_inc(route, 1)
                dve.wait_ge(route, r + 1)
                nc.vector.tensor_tensor(dm[:, :], mx[:, :, 1], mx[:, :, 0], ALU.subtract).then_inc(gap_ready, 1)
                for k in range(K4):
                    ins = nc.vector.max_index(ix[:, k, :], mx[:, k, :], lg[:, k, :])
                ins.then_inc(route, 1)
                dve.wait_ge(route, r + 2)
                nc.vector.tensor_copy(ixf[:, :, :], ix[:, :, 0:2].rearrange("p k j -> p j k")).then_inc(route, 1)
                dve.wait_ge(route, r + 3)
                for j in range(2):
                    ins = nc.vector.tensor_tensor(oh[:, j, :, :], iota8[:, :].unsqueeze(1).to_broadcast([P, K4, E]),
                                                  ixf[:, j, :].unsqueeze(2).to_broadcast([P, K4, E]), ALU.is_equal)
                ins.then_inc(route, 1)

            def route_second(L, b):
                r = b * ROUTE + NB * L * ROUTE
                dve.wait_ge(exp_ready, b + (NB * L + 1))
                nc.vector.tensor_scalar(sm[:, :], ex[:, :], 1.0, None, ALU.add).then_inc(route, 1)
                dve.wait_ge(route, r + 5)
                nc.vector.reciprocal(wp[:, 0, :], sm[:, :]).then_inc(route, 1)
                dve.wait_ge(route, r + 6)
                nc.vector.tensor_tensor(wp[:, 1, :], wp[:, 0, :], ex[:, :], ALU.mult).then_inc(route, 1)
                dve.wait_ge(route, r + 7)
                v = oh[:, :, :, :].rearrange("p j k e -> p (j k) e")
                w = wp[:, :, :].rearrange("p j k -> p (j k)")
                nc.vector.tensor_tensor(v, v, w.unsqueeze(2).to_broadcast([P, 2 * K4, E]), ALU.mult).then_inc(route, 1)
                dve.wait_ge(route, r + 8)
                nc.vector.tensor_tensor(wf[:, :, :], oh[:, 0, :, :], oh[:, 1, :, :], ALU.add).then_inc(route, 1)
                dve.wait_ge(route, r + 9)
                nc.vector.tensor_copy(wh[:, :, :], wf[:, :, :]).then_inc(route, 1)
                dve.wait_ge(route, r + 10)
                nc.vector.tensor_copy(wcat[:, :, 0:E], wh[:, :, :].bitcast(F32))
                nc.vector.tensor_tensor(wcat[:, :, E:2 * E], wf[:, :, :], wh[:, :, :].bitcast(F32),
                                        ALU.subtract).then_inc(gates_ready, 1)

            def add_experts(L, b):
                u = m_end(L, b, 0)
                dve.wait_ge(m_ready, u + 1)
                nc.vector.tensor_tensor(X[:, blk(b)], MB, X[:, blk(b)], ALU.add).then_inc(m_free, 1)
                if L == 0:
                    dve.wait_ge(m_free, u + 1)
                    norm_stats(n_end(L, b), X_rows(b))

            def message_out(b):
                dve.wait_ge(m_ready, m_end(0, b, 2) + 1)
                nc.vector.tensor_tensor(MSG[:, blk(b)].rearrange("p (k d) -> p k d", d=D),
                                        MB.rearrange("p (k d) -> p k d", d=D),
                                        Bm[:, :].unsqueeze(1).to_broadcast([P, K4, D]), ALU.add).then_inc(m_free, 1)

            def experts(L):
                add_graph(L, 0)
                first_norm(L, 0)
                if L == 0:
                    second_norm(L, 0)
                low_part(L, 0, 0)
                route_first(L, 0)
                route_second(L, 0)

                def body(b, par):
                    more = not last(b)
                    for e in range(E):
                        gate_hidden(L, b, e)
                        if e == 0 and not first(b):
                            add_experts(L, b - 1)
                        if e == 1 and not first(b) and L == 0:
                            normalise(n_end(L, b - 1), X_rows(b - 1))
                        if e == 2 and not first(b) and L == 0:
                            message_out(b - 1)
                        if e == 3 and more:
                            add_graph(L, b + 1)
                        if e == 4 and more:
                            first_norm(L, b + 1)
                        if e == 5 and more and L == 0:
                            second_norm(L, b + 1)
                        if e == 6 and more:
                            low_part(L, b + 1, 1 - par)
                            route_first(L, b + 1)
                        if e == 7 and more:
                            route_second(L, b + 1)

                blocks(dve, body)
                add_experts(L, NB - 1)
                if L == 0:
                    normalise(n_end(L, NB - 1), X_rows(NB - 1))
                    message_out(NB - 1)

            experts(0)

            def mask(u, s, arrivals):
                dve.wait_ge(loaded2[s], arrivals * 16)
                nc.vector.scalar_tensor_tensor(ring[s][:, :], ring[s][:, :], CUTOFF, ring[s][:, :],
                                               ALU.is_lt, ALU.mult).then_inc(masked, 1)

            def square_streamed(u, s):
                dve.wait_ge(inverse, u + 1)
                nc.vector.scalar_tensor_tensor(ring[s][:, :], ring[s][:, :], 2.0, ring[s][:, :],
                                               ALU.subtract, ALU.mult).then_inc(square, 1)

            def stream(g):
                for s in range(S2):
                    mask(g * S2 + s, s, g + 1)
                    if not (first(g) and s == 0):
                        square_streamed(g * S2 + (s - 1), (s - 1) % S2)

            stream(0)
            with dve.Fori(1, NG) as g:
                stream(g)
            for s in range(2):
                mask(NG * S2 + s, s, NG + 1)
                square_streamed(NG * S2 + s - 1, (s - 1) % S2)
            square_streamed(NG * S2 + 1, 1)
            split_weights(1)
            dve.wait_ge(prod2, T + 2)
            for b in range(4, 8):
                nc.vector.tensor_copy(AG[:, b * BK:(b + 1) * BK], bank[:, b, :]).then_inc(evac2, 1)
            experts(1)

        @block.scalar
        def _(act):
            for dst, src in params:
                act.dma_start(dst, src).then_inc(params_in, 16)
            act.sem_inc(acted, 4)
            act.preload_act_table_set("natural_log_exp_and_others")
            act.wait_ge(consts, 8)

            for g in range(NG):
                v = C[:, g * N:(g + 1) * N]
                act.wait_ge(c_masked, g + 1)
                nc.scalar.activation(v, v, ACT.Ln, bias=tiny[:, :]).then_inc(c_log, 1)
                act.wait_ge(c_log, g + 1)
                nc.scalar.activation(v, v, ACT.Exp, scale=-1.0).then_inc(c_inverse, 1)
                act.wait_ge(c_square, g + 1)
                nc.scalar.activation(v, v, ACT.Exp, scale=-2.0, bias=minus2[:, :]).then_inc(c_ready, 1)
            act.wait_ge(prod1, T + S1)
            for b in range(4):
                nc.scalar.activation(AG[:, b * BK:(b + 1) * BK], bank[:, b, :], ACT.Copy).then_inc(evac1, 1)

            def hidden(L, b, e):
                n = expert_no(L, b, e)
                s = e % 2
                act.wait_ge(w2_done, n + 1)
                for c in range(HC):
                    act.wait_ge(hid_ready, n * 2 + (c + 1))
                    nc.scalar.activation(hid[s][:, c, :], HB[s][:, c, :], ACT.Gelu if L == 0 else ACT.Relu,
                                         bias=b1t[L][:, e * HC + c:e * HC + c + 1]).then_inc(acted, 1)

            def transposed_rows(L, b, par):
                u = m_pre(L, b, 1)
                act.wait_ge(m_ready, u + 1)
                if L == 0:
                    nc.scalar.activation(xT[:, :], MB, ACT.Identity, scale=gam[:, :], bias=bet[:, :]).then_inc(m_free, 1)
                else:
                    nc.scalar.activation(xT[:, :], MB, ACT.Copy).then_inc(m_free, 1)
                act.wait_ge(m_free, u + 1)
                nc.scalar.activation(XTh[par][:, :], xT[:, :], ACT.Copy).then_inc(xh_ready, 1)

            def transposed_gates(L, b, par):
                act.wait_ge(m_ready, m_pre(L, b, 3) + 1)
                nc.scalar.activation(wT[par][:, :], MB[0:2 * E, :], ACT.Copy).then_inc(m_free, 1)

            def message_rows(b):
                act.wait_ge(m_ready, m_end(0, b, 1) + 1)
                nc.scalar.activation(xT[:, :], MB, ACT.Copy).then_inc(m_free, 1)

            def experts(L):
                transposed_rows(L, 0, 0)
                transposed_gates(L, 0, 0)
                hidden(L, 0, 0)

                def body(b, par):
                    more = not last(b)
                    for e in range(E):
                        if e < E - 1:
                            hidden(L, b, e + 1)
                        elif more:
                            hidden(L, b + 1, 0)
                        if e == 1 and not first(b) and L == 0:
                            message_rows(b - 1)
                        if e == 5 and more:
                            transposed_rows(L, b + 1, 1 - par)
                        if e == 7 and more:
                            transposed_gates(L, b + 1, 1 - par)
                    act.wait_ge(w2_done, expert_no(L, b, E - 1) + 3)
                    nc.scalar.activation(YS[:, :], YB, ACT.Copy).then_inc(y_out, 1)

                blocks(act, body)
                if L == 0:
                    message_rows(NB - 1)

            experts(0)

            act.preload_act_table_set("natural_log_exp_and_others")

            def invert(u, s):
                act.wait_ge(masked, u + 1)
                nc.scalar.activation(ring[s][:, :], ring[s][:, :], ACT.Ln, bias=tiny[:, :]).then_inc(logged, 1)
                act.wait_ge(logged, u + 1)
                nc.scalar.activation(ring[s][:, :], ring[s][:, :], ACT.Exp, scale=-1.0).then_inc(inverse, 1)

            def sensitivity(u, s):
                act.wait_ge(square, u + 1)
                nc.scalar.activation(ring[s][:, :], ring[s][:, :], ACT.Exp, scale=-2.0,
                                     bias=minus2[:, :]).then_inc(f_ready, 1)

            def stream(g):
                for s in range(S2):
                    invert(g * S2 + s, s)
                    if not (first(g) and s == 0):
                        sensitivity(g * S2 + (s - 1), (s - 1) % S2)

            stream(0)
            with act.Fori(1, NG) as g:
                stream(g)
            for s in range(2):
                invert(NG * S2 + s, s)
                sensitivity(NG * S2 + s - 1, (s - 1) % S2)
            sensitivity(NG * S2 + 1, 1)
            act.wait_ge(prod2, T + 2)
            for b in range(4):
                nc.scalar.activation(AG[:, b * BK:(b + 1) * BK], bank[:, b, :], ACT.Copy).then_inc(evac2, 1)
            experts(1)

        @block.tensor
        def _(pe):
            pe.sem_inc(prod1, S1)
            pe.sem_inc(w2_done, 2)
            pe.sem_inc(prod2, 2)

            def product(xslot, adj, start, stop):
                for b in range(NB):
                    ins = nc.tensor.matmul(bank[:, b, :], xs[xslot][:, :], adj[:, b * BK:(b + 1) * BK],
                                           start=start, stop=stop)
                return ins

            def graph1(t, s, xslot, start=False, stop=False):
                pe.wait_ge(tile_ready, t + 1)
                product(xslot, ring[s], start, stop).then_inc(prod1, 1)

            graph1(0, 0, 0, start=True)
            with pe.Fori(0, NG) as g:
                for k in range(G):
                    t = 1 + k
                    graph1(g * G + t, t % S1, t % 2)
            graph1(T - 1, (T - 1) % S1, (T - 1) % 2, stop=True)
            pe.wait_ge(summed, T + S1)
            pe.wait_ge(evac1, NB)
            for t in range(T):
                ins = nc.tensor.matmul(MB[:, t:t + 1], colsum[:, t * P:(t + 1) * P], ones[:, :], start=True, stop=True)
            ins.then_inc(sums_ready, 1)

            def graph_rows(L, b):
                pe.wait_ge(staged, b + (NB * L + 1))
                u = m_pre(L, b, 0)
                if first(b) and L == 0:
                    pe.wait_ge(scl_ready, 1)
                else:
                    pe.wait_ge(m_free, u)
                for k in range(K4):
                    a = AGS[:, k * P:(k + 1) * P]
                    if L == 0:
                        ins = nc.tensor.matmul(MB[:, k * P:(k + 1) * P], a, Kw[:, :], start=True, stop=True)
                    else:
                        ins = nc.tensor.transpose(MB[:, k * P:(k + 1) * P], a, ident[:, :])
                ins.then_inc(m_ready, 1)

            def transpose_rows(n, u):
                pe.wait_ge(normed, n + 1)
                pe.wait_ge(m_free, u)
                for k in range(K4):
                    ins = nc.tensor.transpose(MB[:, k * P:(k + 1) * P], XL[:, k * P:(k + 1) * P], ident[:, :])
                ins.then_inc(m_ready, 1)

            def logits(L, b):
                pe.wait_ge(m_free, m_pre(L, b, 2))
                for k in range(K4):
                    ins = nc.tensor.matmul(MB[:, k * E:(k + 1) * E], xT[:, k * P:(k + 1) * P], Wrt[L][:, :],
                                           start=True, stop=True)
                ins.then_inc(m_ready, 1)

            def transpose_gates(L, b):
                pe.wait_ge(gates_ready, b + (NB * L + 1))
                pe.wait_ge(m_free, m_pre(L, b, 3))
                for k in range(K4):
                    ins = nc.tensor.matmul(MB[0:2 * E, k * P:(k + 1) * P], wcat[:, k, :], ident[:, :],
                                           start=True, stop=True)
                ins.then_inc(m_ready, 1)

            def transpose_output(L, b):
                pe.wait_ge(y_out, b + (NB * L + 1))
                pe.wait_ge(m_free, m_end(L, b, 0))
                for k in range(K4):
                    ins = nc.tensor.transpose(MB[:, k * P:(k + 1) * P], YS[:, k * P:(k + 1) * P], ident[:, :])
                ins.then_inc(m_ready, 1)

            def messages(b):
                pe.wait_ge(m_free, m_end(0, b, 2))
                for k in range(K4):
                    ins = nc.tensor.matmul(MB[:, k * P:(k + 1) * P], xT[:, k * P:(k + 1) * P], Wm[:, :],
                                           start=True, stop=True)
                ins.then_inc(m_ready, 1)

            def up(L, b, e, par):
                n = expert_no(L, b, e)
                s = e % 2
                if e == 0:
                    pe.wait_ge(xt_ready, b + (NB * L + 1))
                for c in range(HC):
                    pe.wait_ge(acted, n * 2 + (c + 1))
                    w = slice((e * HC + c) * P, (e * HC + c + 1) * P)
                    nc.tensor.matmul(HB[s][:, c, :], W1h[L][:, w], XTh[par][:, :], start=True, stop=False)
                    nc.tensor.matmul(HB[s][:, c, :], W1h[L][:, w], XTl[par][:, :], start=False, stop=False)
                    nc.tensor.matmul(HB[s][:, c, :], W1l[L][:, w], XTh[par][:, :], start=False,
                                     stop=True).then_inc(hid_ready, 1)

            def gate(L, b, e, par):
                if e == 0:
                    pe.wait_ge(m_free, m_pre(L, b, 3) + 1)
                pe.wait_ge(gated, expert_no(L, b, e) + 1)
                nc.tensor.matmul(GB[e % 2], sel[:, e * P:(e + 1) * P], wT[par][:, :], start=True,
                                 stop=True).then_inc(gb_ready, 1)

            def output_bias(L, b, par):
                if not (first(b) and L == 0):
                    pe.wait_ge(y_out, b + NB * L)
                nc.tensor.matmul(YB, b2h[L][:, :], wT[par][:, :], start=True, stop=False)
                nc.tensor.matmul(YB, b2l[L][:, :], wT[par][:, :], start=False, stop=False)

            def down(L, b, e):
                pe.wait_ge(gated, expert_no(L, b, e) + 3)
                for c in range(HC):
                    ins = nc.tensor.matmul(YB, W2[L][:, (e * HC + c) * D:(e * HC + c + 1) * D], hid[e % 2][:, c, :],
                                           start=False, stop=(e == E - 1 and c == HC - 1))
                ins.then_inc(w2_done, 1)

            def experts(L):
                graph_rows(L, 0)
                transpose_rows(n_pre(L, 0, N_PRE[L] - 1), m_pre(L, 0, 1))
                logits(L, 0)
                transpose_gates(L, 0)
                pe.wait_ge(split_done, 2 * L + 2)
                up(L, 0, 0, 0)
                gate(L, 0, 0, 0)

                def body(b, par):
                    more = not last(b)
                    for e in range(E):
                        if e < E - 1:
                            up(L, b, e + 1, par)
                        elif more:
                            up(L, b + 1, 0, 1 - par)
                        if e == 0:
                            output_bias(L, b, par)
                        down(L, b, e)
                        if e < E - 1:
                            gate(L, b, e + 1, par)
                        if e == 0 and not first(b):
                            transpose_output(L, b - 1)
                        if e == 1 and not first(b) and L == 0:
                            transpose_rows(n_end(L, b - 1), m_end(L, b - 1, 1))
                        if e == 2 and not first(b) and L == 0:
                            messages(b - 1)
                        if e == 3 and more:
                            graph_rows(L, b + 1)
                        if e == 5 and more:
                            transpose_rows(n_pre(L, b + 1, N_PRE[L] - 1), m_pre(L, b + 1, 1))
                        if e == 6 and more:
                            logits(L, b + 1)
                        if e == 7 and more:
                            transpose_gates(L, b + 1)
                            gate(L, b + 1, 0, 1 - par)

                blocks(pe, body)
                transpose_output(L, NB - 1)
                if L == 0:
                    transpose_rows(n_end(L, NB - 1), m_end(L, NB - 1, 1))
                    messages(NB - 1)

            experts(0)
            pe.wait_ge(m_free, M_ALL)
            pe.wait_ge(y_out, NB)
            pe.wait_ge(c_ready, NG)

            def graph2_cached(g, start=False):
                pe.wait_ge(msg_staged, g * G + 1)
                for b in range(NB):
                    ins = nc.tensor.matmul(bank[:, b, :], xs[0][:, :], C[:, bass.ds(g * N + b * BK, BK)],
                                           start=start, stop=False)
                ins.then_inc(prod2, 1)

            def graph2_streamed(k, u, s, stop=False):
                pe.wait_ge(msg_staged, k + 1)
                pe.wait_ge(f_ready, u + 1)
                product(1 - s % 2, ring[s], False, stop).then_inc(prod2, 1)

            def group(g, start=False):
                graph2_cached(g, start)
                for s in range(S2):
                    graph2_streamed(g * G + (1 + s), g * S2 + s, s)

            group(0, start=True)
            with pe.Fori(1, NG) as g:
                group(g)
            for s in range(2):
                pe.wait_ge(msg_staged, T - 1 + s)
                pe.wait_ge(f_ready, NG * S2 + s + 1)
                product(s, ring[s], False, s == 1).then_inc(prod2, 1)
            pe.wait_ge(evac2, NB)
            experts(1)


def kernel(x, adj, L0_gnn_kernel, L0_gnn_bias, L0_gnn_beta, L0_ffn_gamma, L0_ffn_beta, L0_ffn_Wr, L0_ffn_br,
           L0_ffn_W1, L0_ffn_b1, L0_ffn_W2, L0_ffn_b2, L1_gnn_W, L1_gnn_B, L1_ffn_Wg, L1_ffn_bg, L1_ffn_bias,
           L1_ffn_W1, L1_ffn_b1, L1_ffn_W2, L1_ffn_b2):
    import numpy as np
    import concourse.bacc as bacc
    from concourse import mybir as mb
    from concourse.bass_utils import run_bass_kernel_spmd

    N, D = np.shape(x)
    P = 128

    def rows(a):
        return np.asarray(a).reshape(N // P, P, D).transpose(1, 0, 2).reshape(P, -1)

    def up(w):
        return np.asarray(w).transpose(1, 0, 2).reshape(D, -1)

    def chunks(w):
        w = np.asarray(w)
        return w.reshape(w.shape[0], w.shape[1] // P, P, -1).transpose(2, 0, 1, 3).reshape(P, -1)

    ins = {
        "x_t": rows(x), "adj_t": np.asarray(adj).T, "kern0": L0_gnn_kernel, "bias0": L0_gnn_bias,
        "beta_t": np.asarray(L0_gnn_beta).reshape(N // P, P).T,
        "gamma": np.asarray(L0_ffn_gamma).reshape(D, 1), "beta_ln": np.asarray(L0_ffn_beta).reshape(D, 1),
        "wr": L0_ffn_Wr, "br": L0_ffn_br, "w1a": up(L0_ffn_W1), "b1a": chunks(L0_ffn_b1),
        "w2a": chunks(L0_ffn_W2), "b2a": L0_ffn_b2, "wm": L1_gnn_W, "bm": L1_gnn_B,
        "wg": L1_ffn_Wg, "bg": L1_ffn_bg, "gate_bias": L1_ffn_bias, "w1b": up(L1_ffn_W1),
        "b1b": chunks(L1_ffn_b1), "w2b": chunks(L1_ffn_W2), "b2b": L1_ffn_b2,
    }
    nc = bacc.Bacc("TRN2", target_bir_lowering=False, num_devices=1)
    arrays, args = {}, []
    for name, a in ins.items():
        a = np.ascontiguousarray(a)
        arrays[f"in_{name}"] = a
        args.append(nc.dram_tensor(f"in_{name}", a.shape, mb.dt.from_np(a.dtype), kind="ExternalInput").ap())
    args.append(nc.dram_tensor("out_x", (P, N), mb.dt.float32, kind="ExternalOutput").ap())
    gnn_moe_two_layers(nc, *args)
    r = run_bass_kernel_spmd(nc, [arrays], core_ids=[0])
    got = r.results[0]["out_x"]
    return got.reshape(P, N // P, D).transpose(1, 0, 2).reshape(N, D)
```

```python
import concourse.bass as bass
from concourse import mybir
from contextlib import ExitStack


def gnn_moe_two_layers(nc, x_t, adj_t, kern0, bias0, beta_t, gamma, beta_ln, wr, br, w1a, b1a, w2a, b2a,
                       wm, bm, wg, bg, gate_bias, w1b, b1b, w2b, b2b, out):
    F32, F32R, U32 = mybir.dt.float32, mybir.dt.float32r, mybir.dt.uint32
    ALU, ACT = mybir.AluOpType, mybir.ActivationFunctionType

    P = 128
    N = adj_t.shape[0]
    D = kern0.shape[0]
    E = wr.shape[1]
    H = w1a.shape[1] // E
    HC = H // P
    T = N // P
    BK = 512
    NB = N // BK
    K4 = BK // P
    EPS = 1e-5
    G = 6
    NG = 5
    S1 = 3
    S2 = 5
    assert D == P and T == G * NG + 2 and NB == 8 and HC == 2 and E == 8
    CUTOFF = 1.0
    TINY = 1e-18

    ctx = ExitStack()
    with ctx:
        def sb(name, shape, dt=F32):
            return ctx.enter_context(nc.sbuf_tensor(name, shape, dt))

        def sem(name):
            return ctx.enter_context(nc.semaphore(name))

        TB = N * 4
        ARENA = (nc.sbuf_base + 31) // 32 * 32
        sb("arena", [P, (1 + NG + S2 + 1) * N + 8])

        def at(name, offset, shape, dt=F32):
            return nc.alloc_sbuf_tensor_at(name, shape, dt, offset=offset)

        R_C = ARENA + TB
        R_R = R_C + NG * TB
        R_A = R_R + S2 * TB
        X = at("X", ARENA, [P, N])
        seed = at("seed", R_C + (NG - 1) * TB, [2 * E, E * P])
        C = at("C", R_C, [P, NG * N])
        ring = [at(f"ring{s}", R_R + s * TB, [P, N]) for s in range(1, S2)]
        ring.insert(0, at("ring0", R_A, [P, N]))
        AG = at("AG", R_R, [P, N])
        MSG = at("MSG", R_R, [P, N])
        ring1 = [at("ring1_0", R_R, [P, N]), ring[3], ring[4]]
        colsum = at("colsum", R_A, [P, N])
        BB = BK * 4
        o = R_R + 3 * TB
        NP = 4
        hid = [at(f"hid{s}", o + s * HC * BB, [P, HC, BK]) for s in range(NP)]
        hlo = [at(f"hlo{s}", o + s * HC * BB, [P, HC, BK], F32R) for s in range(NP)]
        hhi = [at(f"hhi{s}", R_A + s * HC * BB, [P, HC, BK], F32R) for s in range(2)]
        XTh = [at(f"XTh{s}", R_A + (4 + s) * BB, [P, BK], F32R) for s in range(2)]
        XTl = [at(f"XTl{s}", R_A + (6 + s) * BB, [P, BK], F32R) for s in range(2)]
        o = R_R + 4 * TB
        XL = at("XL", o, [P, BK])
        XLe = at("XLe", o + BB, [P, BK])
        YS = at("YS", o + 2 * BB, [P, BK])
        AGS = at("AGS", o + 3 * BB, [P, BK])
        xT = at("xT", o + 4 * BB, [P, BK])
        xTe = at("xTe", o + 5 * BB, [P, BK])
        wT = [at(f"wT{s}", o + (6 + s) * BB, [2 * E, BK], F32R) for s in range(2)]
        WBY = E * H * 4
        W1h, W1l, W1raw, W2h, W2l, W2raw = [], [], [], [], [], []
        for L, o in ((0, R_R + TB), (1, R_C)):
            for name, hi, lo, raw, k in (("W1", W1h, W1l, W1raw, 0), ("W2", W2h, W2l, W2raw, 2)):
                hi.append(at(f"{name}h{L}", o + k * WBY, [P, E * H], F32R))
                lo.append(at(f"{name}l{L}", o + (k + 1) * WBY, [P, E * H], F32R))
                raw.append(at(f"{name}raw{L}", o + (k + 1) * WBY, [P, E * H]))

        sel = sb("sel", [2 * E, E * P], F32R)
        ident = sb("ident", [P, P])
        Kw = sb("Kw", [P, D])
        Wm = sb("Wm", [P, D])
        Bm = sb("Bm", [P, D])
        B0 = sb("B0", [P, D])
        Wrt = [sb("Wr", [P, E]), sb("Wg", [P, E])]
        brt = [sb("br_bc", [P, E]), sb("bg_bc", [P, E])]
        gb_bc = sb("gb_bc", [P, E])
        gam = sb("gam", [P, 1])
        bet = sb("bet", [P, 1])
        b1t = [sb("b1_0", [P, E * HC]), sb("b1_1", [P, E * HC])]
        b2r = [sb("b2r0", [2 * E, D]), sb("b2r1", [2 * E, D])]
        b2h = [sb("b2h0", [2 * E, D], F32R), sb("b2h1", [2 * E, D], F32R)]
        b2l = [sb("b2l0", [2 * E, D], F32R), sb("b2l1", [2 * E, D], F32R)]
        btile = sb("btile", [P, T])
        scl = sb("scl", [P, T])
        ones = sb("ones", [P, 1])
        scratch = sb("scratch", [P, 1])
        tiny = sb("tiny", [P, 1])
        minus2 = sb("minus2", [P, 1])
        nhalf = sb("nhalf", [P, 8])
        euler = sb("euler", [P, K4])
        iota8 = sb("iota8", [P, E])
        xs = [sb(f"xs{s}", [P, D]) for s in range(2)]
        st = sb("st", [P, 8, 6])
        ste = sb("ste", [P, K4, 6])
        mve = sb("mve", [P, K4, 2])
        vee = sb("vee", [P, K4])
        rse = sb("rse", [P, K4])
        mv = sb("mv", [P, T, 2])
        ve = sb("ve", [P, T])
        rs = sb("rs", [P, T])
        lg = sb("lg", [P, K4, E])
        mx = sb("mx", [P, K4, 8])
        ix = sb("ix", [P, K4, 8], U32)
        ixf = sb("ixf", [P, 2, K4])
        dm = sb("dm", [P, K4])
        ex = sb("ex", [P, K4])
        sm = sb("sm", [P, K4])
        wp = sb("wp", [P, 2, K4])
        oh = sb("oh", [P, 2, K4, E])
        wf = sb("wf", [P, K4, E])
        wh = sb("wh", [P, K4, E], F32R)
        wcat = sb("wcat", [P, K4, 2 * E])

        bank = ctx.enter_context(nc.psum_tensor("bank", [P, 8, BK], F32))
        HB = [bank[:, 2 * s:2 * s + 2, :] for s in range(2)]
        YB = bank[:, 4, :]
        GB = bank[:, 5, :]
        MP = bank[:, 6, :]
        ME = bank[:, 7, :]

        x_in = [sem(f"x_in{c}") for c in range(4)]
        beta_in = sem("beta_in")
        params_in = sem("params_in")
        w_in = [sem("w_in0"), sem("w_in1")]
        loaded1 = [sem(f"loaded1_{s}") for s in range(S1)]
        loaded2 = [sem(f"loaded2_{s}") for s in range(S2)]
        consts = sem("consts")
        smalls = sem("smalls")
        stats_done = sem("stats_done")
        aggr_done = sem("aggr_done")
        var_ready = sem("var_ready")
        rstd_ready = sem("rstd_ready")
        normed = sem("normed")
        e_stats = sem("e_stats")
        e_aggr = sem("e_aggr")
        e_var = sem("e_var")
        e_rstd = sem("e_rstd")
        e_normed = sem("e_normed")
        split1 = sem("split1")
        split2 = sem("split2")
        tile_ready = sem("tile_ready")
        summed = sem("summed")
        prod1 = sem("prod1")
        c_masked = sem("c_masked")
        c_log = sem("c_log")
        c_inverse = sem("c_inverse")
        c_square = sem("c_square")
        c_ready = sem("c_ready")
        biased = sem("biased")
        evac_a = [sem("evac_a0"), sem("evac_a1")]
        evac_v = [sem("evac_v0"), sem("evac_v1")]
        sums_ready = sem("sums_ready")
        scl_ready = sem("scl_ready")
        staged = sem("staged")
        mp_ready = sem("mp_ready")
        mp_free = sem("mp_free")
        me_ready = sem("me_ready")
        me_free = sem("me_free")
        xh_ready = sem("xh_ready")
        xt_ready = sem("xt_ready")
        route = sem("route")
        gap_ready = sem("gap_ready")
        exp_ready = sem("exp_ready")
        gates_ready = sem("gates_ready")
        hi_ready = sem("hi_ready")
        lo_ready = sem("lo_ready")
        hid_ready = sem("hid_ready")
        acted = sem("acted")
        gb_ready = sem("gb_ready")
        gated = sem("gated")
        w2_done = sem("w2_done")
        y_out = sem("y_out")
        masked = sem("masked")
        logged = sem("logged")
        inverse = sem("inverse")
        square = sem("square")
        f_ready = sem("f_ready")
        msg_staged = sem("msg_staged")
        prod2 = sem("prod2")
        stored = sem("stored")

        def tile(t):
            return bass.ds(t * P, P)

        def blk(b):
            return bass.ds(b * BK, BK)

        M_PRE, M_END = 4, (3, 1)
        N_FIRST = 4
        ROUTE = 10

        def mp_no(L, b, k):
            return b * M_PRE + (L * NB * M_PRE + k)

        def me_no(L, b, k):
            return b * M_END[L] + (L * NB * M_END[0] + k)

        def n_no(L, b):
            return b + L * NB

        def expert_no(L, b, e):
            return b * E + (L * NB * E + e)

        def blocks(eng, body):
            body(0, 0)
            with eng.Fori(0, (NB - 2) // 2) as g:
                body(g * 2 + 1, 1)
                body(g * 2 + 2, 0)
            body(NB - 1, 1)

        def ahead_of(b, e, par, steps):
            if e + steps < E:
                return b, e + steps, par
            return None if last(b) else (b + 1, e + steps - E, 1 - par)

        def first(b):
            return isinstance(b, int) and b == 0

        def last(b):
            return isinstance(b, int) and b == NB - 1

        params = [(Kw[:, :], kern0), (Wm[:, :], wm), (Bm[:, :], bm.partition_broadcast(P)),
                  (B0[:, :], bias0.partition_broadcast(P)), (Wrt[0][:, :], wr), (Wrt[1][:, :], wg),
                  (brt[0][:, :], br.partition_broadcast(P)), (brt[1][:, :], bg.partition_broadcast(P)),
                  (gb_bc[:, :], gate_bias.partition_broadcast(P)), (gam[:, :], gamma), (bet[:, :], beta_ln),
                  (b1t[0][:, :], b1a), (b1t[1][:, :], b1b)]
        for L, b2 in ((0, b2a), (1, b2b)):
            params += [(b2r[L][0:E, :], b2), (b2r[L][E:2 * E, :], b2)]
        PARAMS = len(params)

        block = ctx.enter_context(nc.Block())

        @block.sync
        def _(sp):
            def load_x(c):
                sp.dma_start(X[:, c * 8 * P:(c + 1) * 8 * P], x_t[:, c * 8 * P:(c + 1) * 8 * P]).then_inc(x_in[c], 16)

            def load1(t, s):
                sp.wait_ge(prod1, t + 1)
                sp.wait_ge(summed, t + 1)
                sp.dma_start(ring1[s][:, :], adj_t[tile(t), :]).then_inc(loaded1[s], 16)

            load_x(0)
            load1(0, 0)
            for c in range(1, 4):
                load_x(c)
            sp.dma_start(W1raw[0][:, :], w1a).then_inc(w_in[0], 16)
            sp.dma_start(W2raw[0][:, :], w2a).then_inc(w_in[0], 16)
            with sp.Fori(0, NG) as g:
                for k in range(G):
                    load1(g * G + (1 + k), (1 + k) % S1)
            load1(T - 1, (T - 1) % S1)
            def load2(t, s):
                sp.dma_start(ring[s][:, :], adj_t[tile(t), :]).then_inc(loaded2[s], 16)

            sp.wait_ge(w2_done, NP + E * NB)
            load2(2, 0)
            load2(3, 1)
            load2(4, 2)
            load2(5, 3)
            sp.wait_ge(me_free, NB * M_END[0])
            load2(6, 4)
            with sp.Fori(1, NG) as g:
                for k in range(1, G):
                    sp.wait_ge(prod2, g * G + (k - G + 3))
                    load2(g * G + (1 + k), k - 1)
            sp.dma_start(W1raw[1][:, :], w1b).then_inc(w_in[1], 16)
            sp.dma_start(W2raw[1][:, :], w2b).then_inc(w_in[1], 16)
            for s, t in ((0, 0), (1, T - 1)):
                sp.wait_ge(prod2, (NG - 1) * G + (s + 1) + 3)
                load2(t, s)

            def store(b):
                sp.wait_ge(me_free, me_no(1, b, 0) + 1)
                sp.dma_start(out[:, blk(b)], X[:, blk(b)]).then_inc(stored, 16)

            with sp.Fori(0, NB - 1) as b:
                store(b)
            store(NB - 1)
            sp.wait_ge(stored, 16 * NB)

        @block.gpsimd
        def _(pool):
            pool.memset(ident[:, :], 0.0).then_inc(consts, 1)
            pool.memset(seed[:, :], 0.0).then_inc(consts, 1)
            pool.memset(ones[:, :], 1.0).then_inc(consts, 1)
            pool.memset(tiny[:, :], TINY).then_inc(consts, 1)
            pool.memset(minus2[:, :], -2.0).then_inc(consts, 1)
            pool.memset(nhalf[:, :], -0.5).then_inc(consts, 1)
            pool.memset(euler[:, :], 2.718281828459045).then_inc(consts, 1)
            pool.iota(iota8[:, :], [[1, E]], base=0, channel_multiplier=0,
                      allow_small_or_imprecise_dtypes=True).then_inc(consts, 1)
            pool.wait_ge(consts, 8)
            pool.affine_select(out=ident[:, :], in_=ident[:, :], compare_op=ALU.not_equal, fill=1.0, base=0,
                               pattern=[[-1, P]], channel_multiplier=1).then_inc(consts, 1)
            v = seed[:, :].rearrange("p (e q) -> p e q", q=P)
            for r in range(2):
                if r:
                    pool.wait_ge(consts, 10)
                pool.affine_select(out=v, in_=v, compare_op=ALU.not_equal, fill=1.0, base=-E * r,
                                   pattern=[[-1, E], [0, P]], channel_multiplier=1).then_inc(consts, 1)

            for c in range(N_FIRST):
                pool.wait_ge(var_ready, c + 1)
                pool.tensor_tensor(rs[:, 8 * c:8 * c + 8], ve[:, 8 * c:8 * c + 8], nhalf[:, :],
                                   ALU.pow).then_inc(rstd_ready, 1)

            def split(L, hi, lo, raw, done):
                pool.wait_ge(w_in[L], 32)
                pool.tensor_copy(hi[:, :], raw[:, :]).then_inc(done, 1)
                pool.wait_ge(done, 2 * L + 1)
                pool.tensor_tensor(lo[:, :], raw[:, :], hi[:, :].bitcast(F32), ALU.subtract).then_inc(done, 1)

            split(0, W1h[0], W1l[0], W1raw[0], split1)
            split(0, W2h[0], W2l[0], W2raw[0], split2)
            pool.wait_ge(params_in, PARAMS * 16)
            for c in range(4):
                pool.wait_ge(tile_ready, 8 * c + 8)
                v = X[:, c * 8 * P:(c + 1) * 8 * P].rearrange("p (t d) -> p t d", d=D)
                pool.tensor_tensor(v, v, B0[:, :].unsqueeze(1).to_broadcast([P, 8, D]), ALU.add).then_inc(biased, 1)

            def power(n):
                pool.wait_ge(var_ready, n + (N_FIRST + 1))
                pool.tensor_tensor(rs[:, 0:K4], ve[:, 0:K4], nhalf[:, 0:K4], ALU.pow).then_inc(rstd_ready, 1)

            def stage(L, b):
                pool.tensor_copy(AGS[:, :], AG[:, blk(b)]).then_inc(staged, 1)

            def end(b):
                pool.wait_ge(e_var, b + 1)
                pool.tensor_tensor(rse[:, :], vee[:, :], nhalf[:, 0:K4], ALU.pow).then_inc(e_rstd, 1)

            def gate_exp(L, b):
                pool.wait_ge(gap_ready, b + (NB * L + 1))
                pool.tensor_tensor(ex[:, :], euler[:, :], dm[:, :], ALU.pow).then_inc(exp_ready, 1)

            def low_hidden(L, b, e):
                n = expert_no(L, b, e)
                pool.wait_ge(hi_ready, n + 1)
                for c in range(HC):
                    pool.tensor_tensor(hlo[e % NP][:, c, :], hid[e % NP][:, c, :], hhi[e % 2][:, c, :].bitcast(F32),
                                       ALU.subtract).then_inc(lo_ready, 1)

            def experts(L):
                pool.wait_ge(evac_a[L], 1)
                stage(L, 0)
                power(n_no(L, 0))
                gate_exp(L, 0)
                pool.wait_ge(evac_a[L], 4)
                pool.wait_ge(evac_v[L], 4)
                pool.wait_ge(mp_ready, mp_no(L, 0, 0) + 1)
                stage(L, 1)
                for e in range(2):
                    low_hidden(L, 0, e)

                def body(b, par):
                    for e in range(E):
                        if e == 0 and not last(b):
                            power(n_no(L, b + 1))
                        nxt = ahead_of(b, e, par, 2)
                        if nxt:
                            low_hidden(L, *nxt[:2])
                        if e == 2 and not last(b):
                            gate_exp(L, b + 1)
                        if e == 4 and L == 0 and not first(b):
                            end(b - 1)
                        if e == 5 and not last(b) and not (isinstance(b, int) and b == NB - 2):
                            pool.wait_ge(mp_ready, mp_no(L, b + 1, 0) + 1)
                            stage(L, b + 2)

                body(0, 0)
                with pool.Fori(0, (NB - 4) // 2) as g:
                    body(g * 2 + 1, 1)
                    body(g * 2 + 2, 0)
                body(NB - 3, 1)
                body(NB - 2, 0)
                body(NB - 1, 1)
                if L == 0:
                    end(NB - 1)

            experts(0)

            def message(k, t, s):
                pool.wait_ge(prod2, k + 1)
                pool.tensor_copy(xs[s][:, :], MSG[:, tile(t)]).then_inc(msg_staged, 1)

            pool.wait_ge(me_free, NB * M_END[0])
            with pool.Fori(0, NG) as g:
                for k in range(G):
                    message(g * G + k, g * G + (1 + k), k % 2)
            message(T - 2, 0, 0)
            message(T - 1, T - 1, 1)
            split(1, W1h[1], W1l[1], W1raw[1], split1)
            experts(1)

        @block.vector
        def _(dve):
            def settle():
                nc.vector.memset(scratch[:, :], 0.0)

            def norm_stats(n, src, factor, eps):
                settle()
                for k in range(K4):
                    ins = nc.vector.bn_stats(st[:, k, :], src(k))
                ins.then_inc(stats_done, 1)
                dve.wait_ge(stats_done, n + (N_FIRST + 1))
                settle()
                for k in range(K4):
                    ins = nc.vector.bn_aggr(mv[:, k, :], st[:, k, :])
                ins.then_inc(aggr_done, 1)
                dve.wait_ge(aggr_done, n + (N_FIRST + 1))
                nc.vector.tensor_scalar(ve[:, 0:K4], mv[:, 0:K4, 1], factor, eps, ALU.mult, ALU.add).then_inc(var_ready, 1)

            def normalise(n, src):
                dve.wait_ge(rstd_ready, n + (N_FIRST + 1))
                for k in range(K4):
                    ins = nc.vector.tensor_scalar(XL[:, k * P:(k + 1) * P], src(k), mv[:, k, 0:1], rs[:, k:k + 1],
                                                  ALU.subtract, ALU.mult)
                ins.then_inc(normed, 1)

            def end_stats(b):
                settle()
                for k in range(K4):
                    ins = nc.vector.bn_stats(ste[:, k, :], X[:, tile(b * K4 + k)])
                ins.then_inc(e_stats, 1)
                dve.wait_ge(e_stats, b + 1)
                settle()
                for k in range(K4):
                    ins = nc.vector.bn_aggr(mve[:, k, :], ste[:, k, :])
                ins.then_inc(e_aggr, 1)
                dve.wait_ge(e_aggr, b + 1)
                nc.vector.tensor_scalar(vee[:, :], mve[:, :, 1], EPS, None, ALU.add).then_inc(e_var, 1)

            def end_normalise(b):
                dve.wait_ge(e_rstd, b + 1)
                for k in range(K4):
                    ins = nc.vector.tensor_scalar(XLe[:, k * P:(k + 1) * P], X[:, tile(b * K4 + k)], mve[:, k, 0:1],
                                                  rse[:, k:k + 1], ALU.subtract, ALU.mult)
                ins.then_inc(e_normed, 1)

            def X_rows(b):
                return lambda k: X[:, tile(b * K4 + k)]

            dve.sem_inc(summed, S1)
            dve.sem_inc(gated, 2)

            def first_stats(c):
                dve.wait_ge(x_in[c], 16)
                for k in range(8):
                    t = 8 * c + k
                    ins = nc.vector.bn_stats(st[:, k, :], X[:, t * P:(t + 1) * P])
                ins.then_inc(stats_done, 1)
                dve.wait_ge(stats_done, c + 1)
                for k in range(8):
                    ins = nc.vector.bn_aggr(mv[:, 8 * c + k, :], st[:, k, :])
                ins.then_inc(aggr_done, 1)
                dve.wait_ge(aggr_done, c + 1)
                nc.vector.tensor_scalar(ve[:, 8 * c:8 * c + 8], mv[:, 8 * c:8 * c + 8, 1], EPS, None,
                                        ALU.add).then_inc(var_ready, 1)

            def small_operands():
                dve.wait_ge(params_in, PARAMS * 16)
                for L in range(2):
                    nc.vector.tensor_copy(b2h[L][:, :], b2r[L][:, :]).then_inc(smalls, 1)
                nc.vector.tensor_tensor(brt[1][:, :], brt[1][:, :], gb_bc[:, :], ALU.add).then_inc(smalls, 1)
                dve.wait_ge(smalls, 3)
                for L in range(2):
                    nc.vector.tensor_tensor(b2l[L][:, :], b2r[L][:, :], b2h[L][:, :].bitcast(F32),
                                            ALU.subtract).then_inc(smalls, 1)
                dve.wait_ge(consts, 11)
                nc.vector.tensor_copy(sel[:, :], seed[:, :]).then_inc(smalls, 1)

            first_stats(0)
            dve.wait_ge(beta_in, 16)
            dve.wait_ge(consts, 9)
            dve.wait_ge(rstd_ready, 1)

            def graph1_tile(t, s, xslot, arrivals, cached=None):
                buf = ring1[s]
                dve.wait_ge(loaded1[s], arrivals * 16)
                if cached is not None:
                    nc.vector.scalar_tensor_tensor(C[:, bass.ds(cached * N, N)], buf[:, :], CUTOFF, buf[:, :],
                                                   ALU.is_lt, ALU.mult).then_inc(c_masked, 1)
                dve.wait_ge(prod1, t + 2)
                nc.vector.tensor_scalar(xs[xslot][:, :], X[:, tile(t)], mv[:, bass.ds(t, 1), 0], rs[:, bass.ds(t, 1)],
                                        ALU.subtract, ALU.mult)
                if cached is not None:
                    dve.wait_ge(c_masked, cached + 1)
                nc.vector.scalar_tensor_tensor(buf[:, tile(t)], ident[:, :], btile[:, bass.ds(t, 1)],
                                               buf[:, tile(t)], ALU.mult, ALU.add).then_inc(tile_ready, 1)
                dve.wait_ge(tile_ready, t + 1)
                if first(t):
                    nc.vector.tensor_copy(colsum[:, :], buf[:, :]).then_inc(summed, 1)
                else:
                    dve.wait_ge(summed, t + S1)
                    nc.vector.tensor_tensor(colsum[:, :], colsum[:, :], buf[:, :], ALU.add).then_inc(summed, 1)

            def square_cached(g):
                dve.wait_ge(c_inverse, g + 1)
                v = C[:, bass.ds(g * N, N)]
                nc.vector.scalar_tensor_tensor(v, v, 2.0, v, ALU.subtract, ALU.mult).then_inc(c_square, 1)

            graph1_tile(0, 0, 0, 1)
            first_stats(1)

            def group(g):
                for k in range(G):
                    t = 1 + k
                    graph1_tile(g * G + t, t % S1, t % 2, g * 2 + (t // S1 + 1), g if k == 0 else None)
                    if k == 3:
                        square_cached(g)
                    if first(g) and k in (1, 2):
                        first_stats(1 + k)
                    if first(g) and k == 4:
                        small_operands()
                        dve.wait_ge(rstd_ready, N_FIRST)

            group(0)
            with dve.Fori(1, NG) as g:
                group(g)
            graph1_tile(T - 1, (T - 1) % S1, (T - 1) % 2, (T - 1) // S1 + 1)
            dve.wait_ge(prod1, T + S1)
            for b in range(7, 3, -1):
                nc.vector.tensor_copy(AG[:, b * BK:(b + 1) * BK], bank[:, b, :]).then_inc(evac_v[0], 1)
            dve.wait_ge(sums_ready, 1)
            nc.vector.reciprocal(scl[:, :], ME[:, 0:T]).then_inc(scl_ready, 1)
            dve.wait_ge(scl_ready, 1)
            dve.wait_ge(biased, 4)

            def gate_hidden(L, b, e):
                n = expert_no(L, b, e)
                dve.wait_ge(acted, n * 2 + 6)
                dve.wait_ge(gb_ready, n + 1)
                h = hid[e % NP]
                nc.vector.tensor_tensor(h[:, :, :], h[:, :, :],
                                        GB.unsqueeze(1).to_broadcast([P, HC, BK]), ALU.mult).then_inc(gated, 1)

            def add_graph(L, b):
                u = mp_no(L, b, 0)
                dve.wait_ge(mp_ready, u + 1)
                if L == 0:
                    for k in range(K4):
                        t = b * K4 + k
                        ins = nc.vector.scalar_tensor_tensor(X[:, tile(t)], MP[:, k * P:(k + 1) * P],
                                                             scl[:, bass.ds(t, 1)], X[:, tile(t)], ALU.mult, ALU.add)
                else:
                    ins = nc.vector.tensor_tensor(X[:, blk(b)], MP, X[:, blk(b)], ALU.add)
                ins.then_inc(mp_free, 1)
                dve.wait_ge(mp_free, u + 1)
                if L == 0:
                    norm_stats(n_no(L, b), X_rows(b), 1.0 + EPS, EPS * EPS)
                else:
                    norm_stats(n_no(L, b), X_rows(b), 1.0, EPS)

            def low_part(L, b, par):
                dve.wait_ge(xh_ready, b + (NB * L + 1))
                nc.vector.tensor_tensor(XTl[par][:, :], xT[:, :], XTh[par][:, :].bitcast(F32),
                                        ALU.subtract).then_inc(xt_ready, 1)

            def route_first(L, b):
                u = mp_no(L, b, 2)
                r = b * ROUTE + NB * L * ROUTE
                dve.wait_ge(mp_ready, u + 1)
                nc.vector.tensor_tensor(lg[:, :, :], MP[:, 0:K4 * E].rearrange("p (k e) -> p k e", e=E),
                                        brt[L][:, :].unsqueeze(1).to_broadcast([P, K4, E]), ALU.add).then_inc(mp_free, 1)
                dve.wait_ge(mp_free, u + 1)
                settle()
                for k in range(K4):
                    ins = nc.vector.max(mx[:, k, :], lg[:, k, :])
                ins.then_inc(route, 1)
                dve.wait_ge(route, r + 1)
                nc.vector.tensor_tensor(dm[:, :], mx[:, :, 1], mx[:, :, 0], ALU.subtract).then_inc(gap_ready, 1)
                for k in range(K4):
                    ins = nc.vector.max_index(ix[:, k, :], mx[:, k, :], lg[:, k, :])
                ins.then_inc(route, 1)
                dve.wait_ge(route, r + 2)
                nc.vector.tensor_copy(ixf[:, :, :], ix[:, :, 0:2].rearrange("p k j -> p j k")).then_inc(route, 1)
                dve.wait_ge(route, r + 3)
                for j in range(2):
                    ins = nc.vector.tensor_tensor(oh[:, j, :, :], iota8[:, :].unsqueeze(1).to_broadcast([P, K4, E]),
                                                  ixf[:, j, :].unsqueeze(2).to_broadcast([P, K4, E]), ALU.is_equal)
                ins.then_inc(route, 1)

            def route_second(L, b):
                r = b * ROUTE + NB * L * ROUTE
                dve.wait_ge(exp_ready, b + (NB * L + 1))
                nc.vector.tensor_scalar(sm[:, :], ex[:, :], 1.0, None, ALU.add).then_inc(route, 1)
                dve.wait_ge(route, r + 5)
                nc.vector.reciprocal(wp[:, 0, :], sm[:, :]).then_inc(route, 1)
                dve.wait_ge(route, r + 6)
                nc.vector.tensor_tensor(wp[:, 1, :], wp[:, 0, :], ex[:, :], ALU.mult).then_inc(route, 1)
                dve.wait_ge(route, r + 7)
                v = oh[:, :, :, :].rearrange("p j k e -> p (j k) e")
                w = wp[:, :, :].rearrange("p j k -> p (j k)")
                nc.vector.tensor_tensor(v, v, w.unsqueeze(2).to_broadcast([P, 2 * K4, E]), ALU.mult).then_inc(route, 1)
                dve.wait_ge(route, r + 8)
                nc.vector.tensor_tensor(wf[:, :, :], oh[:, 0, :, :], oh[:, 1, :, :], ALU.add).then_inc(route, 1)
                dve.wait_ge(route, r + 9)
                nc.vector.tensor_copy(wh[:, :, :], wf[:, :, :]).then_inc(route, 1)
                dve.wait_ge(route, r + 10)
                nc.vector.tensor_copy(wcat[:, :, 0:E], wh[:, :, :].bitcast(F32))
                nc.vector.tensor_tensor(wcat[:, :, E:2 * E], wf[:, :, :], wh[:, :, :].bitcast(F32),
                                        ALU.subtract).then_inc(gates_ready, 1)

            def add_experts(L, b):
                u = me_no(L, b, 0)
                dve.wait_ge(me_ready, u + 1)
                nc.vector.tensor_tensor(X[:, blk(b)], ME, X[:, blk(b)], ALU.add).then_inc(me_free, 1)
                if L == 0:
                    dve.wait_ge(me_free, u + 1)
                    end_stats(b)

            def message_out(b):
                dve.wait_ge(me_ready, me_no(0, b, 2) + 1)
                nc.vector.tensor_tensor(MSG[:, blk(b)].rearrange("p (k d) -> p k d", d=D),
                                        ME.rearrange("p (k d) -> p k d", d=D),
                                        Bm[:, :].unsqueeze(1).to_broadcast([P, K4, D]), ALU.add).then_inc(me_free, 1)

            def experts(L):
                add_graph(L, 0)
                normalise(n_no(L, 0), X_rows(0))
                low_part(L, 0, 0)
                route_first(L, 0)
                route_second(L, 0)
                for e in range(2):
                    gate_hidden(L, 0, e)

                def body(b, par):
                    ahead, behind = not last(b), not first(b)
                    for e in range(E):
                        if e == 0 and ahead:
                            add_graph(L, b + 1)
                        if e == 1 and ahead:
                            normalise(n_no(L, b + 1), X_rows(b + 1))
                        nxt = ahead_of(b, e, par, 2)
                        if nxt:
                            gate_hidden(L, *nxt[:2])
                        if e == 2 and ahead:
                            low_part(L, b + 1, 1 - par)
                            route_first(L, b + 1)
                        if e == 3 and ahead:
                            route_second(L, b + 1)
                        if e == 4 and behind:
                            add_experts(L, b - 1)
                        if e == 5 and behind and L == 0:
                            end_normalise(b - 1)
                        if e == 7 and behind and L == 0:
                            message_out(b - 1)

                blocks(dve, body)
                add_experts(L, NB - 1)
                if L == 0:
                    end_normalise(NB - 1)
                    mask(0, 0, 1)
                    message_out(NB - 1)

            def mask(u, s, arrivals):
                dve.wait_ge(loaded2[s], arrivals * 16)
                nc.vector.scalar_tensor_tensor(ring[s][:, :], ring[s][:, :], CUTOFF, ring[s][:, :],
                                               ALU.is_lt, ALU.mult).then_inc(masked, 1)

            experts(0)

            def square_streamed(u, s):
                dve.wait_ge(inverse, u + 1)
                nc.vector.scalar_tensor_tensor(ring[s][:, :], ring[s][:, :], 2.0, ring[s][:, :],
                                               ALU.subtract, ALU.mult).then_inc(square, 1)

            def stream(g):
                for s in range(S2):
                    if not (first(g) and s == 0):
                        mask(g * S2 + s, s, g + 1)
                    if not (first(g) and s == 0):
                        square_streamed(g * S2 + (s - 1), (s - 1) % S2)

            stream(0)
            with dve.Fori(1, NG) as g:
                stream(g)
            for s in range(2):
                mask(NG * S2 + s, s, NG + 1)
                square_streamed(NG * S2 + s - 1, (s - 1) % S2)
            square_streamed(NG * S2 + 1, 1)
            dve.wait_ge(w_in[1], 32)
            nc.vector.tensor_copy(W2h[1][:, :], W2raw[1][:, :]).then_inc(split2, 1)
            dve.wait_ge(split2, 3)
            nc.vector.tensor_tensor(W2l[1][:, :], W2raw[1][:, :], W2h[1][:, :].bitcast(F32),
                                    ALU.subtract).then_inc(split2, 1)
            dve.wait_ge(prod2, T + 2)
            for b in range(7, 3, -1):
                nc.vector.tensor_copy(AG[:, b * BK:(b + 1) * BK], bank[:, b, :]).then_inc(evac_v[1], 1)
            experts(1)

        @block.scalar
        def _(act):
            act.dma_start(btile[:, :], beta_t).then_inc(beta_in, 16)
            for dst, src in params:
                act.dma_start(dst, src).then_inc(params_in, 16)
            act.sem_inc(acted, 4)
            act.preload_act_table_set("natural_log_exp_and_others")
            act.wait_ge(consts, 8)

            for g in range(NG):
                v = C[:, g * N:(g + 1) * N]
                act.wait_ge(c_masked, g + 1)
                nc.scalar.activation(v, v, ACT.Ln, bias=tiny[:, :]).then_inc(c_log, 1)
                act.wait_ge(c_log, g + 1)
                nc.scalar.activation(v, v, ACT.Exp, scale=-1.0).then_inc(c_inverse, 1)
                act.wait_ge(c_square, g + 1)
                nc.scalar.activation(v, v, ACT.Exp, scale=-2.0, bias=minus2[:, :]).then_inc(c_ready, 1)
            act.wait_ge(prod1, T + S1)
            for b in range(4):
                nc.scalar.activation(AG[:, b * BK:(b + 1) * BK], bank[:, b, :], ACT.Copy).then_inc(evac_a[0], 1)

            def hidden(L, b, e):
                n = expert_no(L, b, e)
                act.wait_ge(w2_done, n + 1)
                for c in range(HC):
                    act.wait_ge(hid_ready, n * 2 + (c + 1))
                    nc.scalar.activation(hid[e % NP][:, c, :], HB[e % 2][:, c, :], ACT.Gelu if L == 0 else ACT.Relu,
                                         bias=b1t[L][:, e * HC + c:e * HC + c + 1]).then_inc(acted, 1)

            def high_hidden(L, b, e):
                n = expert_no(L, b, e)
                act.wait_ge(gated, n + 3)
                act.wait_ge(w2_done, n + 3)
                nc.scalar.activation(hhi[e % 2][:, :, :], hid[e % NP][:, :, :], ACT.Copy).then_inc(hi_ready, 1)

            def transposed_rows(L, b, par):
                u = mp_no(L, b, 1)
                act.wait_ge(mp_ready, u + 1)
                if L == 0:
                    nc.scalar.activation(xT[:, :], MP, ACT.Identity, scale=gam[:, :], bias=bet[:, :]).then_inc(mp_free, 1)
                else:
                    nc.scalar.activation(xT[:, :], MP, ACT.Copy).then_inc(mp_free, 1)
                act.wait_ge(mp_free, u + 1)
                nc.scalar.activation(XTh[par][:, :], xT[:, :], ACT.Copy).then_inc(xh_ready, 1)

            def transposed_gates(L, b, par):
                act.wait_ge(mp_ready, mp_no(L, b, 3) + 1)
                nc.scalar.activation(wT[par][:, :], MP[0:2 * E, :], ACT.Copy).then_inc(mp_free, 1)

            def message_rows(b):
                act.wait_ge(me_ready, me_no(0, b, 1) + 1)
                nc.scalar.activation(xTe[:, :], ME, ACT.Copy).then_inc(me_free, 1)

            def invert_first(u, s):
                act.wait_ge(masked, u + 1)
                nc.scalar.activation(ring[s][:, :], ring[s][:, :], ACT.Ln, bias=tiny[:, :]).then_inc(logged, 1)

            def invert_second(u, s):
                act.wait_ge(logged, u + 1)
                nc.scalar.activation(ring[s][:, :], ring[s][:, :], ACT.Exp, scale=-1.0).then_inc(inverse, 1)

            def experts(L):
                transposed_rows(L, 0, 0)
                transposed_gates(L, 0, 0)
                hidden(L, 0, 0)
                hidden(L, 0, 1)
                high_hidden(L, 0, 0)
                hidden(L, 0, 2)
                high_hidden(L, 0, 1)

                def body(b, par):
                    ahead, behind = not last(b), not first(b)
                    for e in range(E):
                        nxt = ahead_of(b, e, par, 3)
                        if nxt:
                            hidden(L, *nxt[:2])
                        nxt = ahead_of(b, e, par, 2)
                        if nxt:
                            high_hidden(L, *nxt[:2])
                        if e == 1 and ahead:
                            transposed_rows(L, b + 1, 1 - par)
                        if e == 4 and ahead:
                            transposed_gates(L, b + 1, 1 - par)
                        if e == 6 and behind and L == 0:
                            message_rows(b - 1)
                    act.wait_ge(w2_done, expert_no(L, b, E - 1) + (NP + 1))
                    nc.scalar.activation(YS[:, :], YB, ACT.Copy).then_inc(y_out, 1)

                blocks(act, body)
                if L == 0:
                    act.preload_act_table_set("natural_log_exp_and_others")
                    invert_first(0, 0)
                    message_rows(NB - 1)
                    invert_second(0, 0)

            experts(0)

            def sensitivity(u, s):
                act.wait_ge(square, u + 1)
                nc.scalar.activation(ring[s][:, :], ring[s][:, :], ACT.Exp, scale=-2.0,
                                     bias=minus2[:, :]).then_inc(f_ready, 1)

            def stream(g):
                for s in range(S2):
                    if not (first(g) and s == 0):
                        invert_first(g * S2 + s, s)
                        invert_second(g * S2 + s, s)
                    if not (first(g) and s == 0):
                        sensitivity(g * S2 + (s - 1), (s - 1) % S2)

            stream(0)
            with act.Fori(1, NG) as g:
                stream(g)
            for s in range(2):
                invert_first(NG * S2 + s, s)
                invert_second(NG * S2 + s, s)
                sensitivity(NG * S2 + s - 1, (s - 1) % S2)
            sensitivity(NG * S2 + 1, 1)
            act.wait_ge(prod2, T + 2)
            for b in range(4):
                nc.scalar.activation(AG[:, b * BK:(b + 1) * BK], bank[:, b, :], ACT.Copy).then_inc(evac_a[1], 1)
            experts(1)

        @block.tensor
        def _(pe):
            pe.sem_inc(prod1, S1)
            pe.sem_inc(w2_done, NP)
            pe.sem_inc(prod2, 2)

            def product(xslot, adj, start, stop):
                for b in range(NB):
                    ins = nc.tensor.matmul(bank[:, b, :], xs[xslot][:, :], adj[:, b * BK:(b + 1) * BK],
                                           start=start, stop=stop)
                return ins

            def graph1(t, s, xslot, start=False, stop=False):
                pe.wait_ge(tile_ready, t + 1)
                product(xslot, ring1[s], start, stop).then_inc(prod1, 1)

            graph1(0, 0, 0, start=True)
            with pe.Fori(0, NG) as g:
                for k in range(G):
                    t = 1 + k
                    graph1(g * G + t, t % S1, t % 2)
            graph1(T - 1, (T - 1) % S1, (T - 1) % 2, stop=True)
            pe.wait_ge(summed, T + S1)
            pe.wait_ge(evac_v[0], 1)
            for t in range(T):
                ins = nc.tensor.matmul(ME[:, t:t + 1], colsum[:, t * P:(t + 1) * P], ones[:, :], start=True, stop=True)
            ins.then_inc(sums_ready, 1)

            def graph_rows(L, b):
                pe.wait_ge(staged, b + (NB * L + 1))
                if not (first(b) and L == 0):
                    pe.wait_ge(mp_free, mp_no(L, b, 0))
                for k in range(K4):
                    a = AGS[:, k * P:(k + 1) * P]
                    if L == 0:
                        ins = nc.tensor.matmul(MP[:, k * P:(k + 1) * P], a, Kw[:, :], start=True, stop=True)
                    else:
                        ins = nc.tensor.transpose(MP[:, k * P:(k + 1) * P], a, ident[:, :])
                ins.then_inc(mp_ready, 1)

            def transpose_rows(L, b):
                pe.wait_ge(normed, n_no(L, b) + 1)
                pe.wait_ge(mp_free, mp_no(L, b, 1))
                for k in range(K4):
                    ins = nc.tensor.transpose(MP[:, k * P:(k + 1) * P], XL[:, k * P:(k + 1) * P], ident[:, :])
                ins.then_inc(mp_ready, 1)

            def logits(L, b):
                pe.wait_ge(mp_free, mp_no(L, b, 2))
                for k in range(K4):
                    ins = nc.tensor.matmul(MP[:, k * E:(k + 1) * E], xT[:, k * P:(k + 1) * P], Wrt[L][:, :],
                                           start=True, stop=True)
                ins.then_inc(mp_ready, 1)

            def transpose_gates(L, b):
                pe.wait_ge(gates_ready, b + (NB * L + 1))
                pe.wait_ge(mp_free, mp_no(L, b, 3))
                for k in range(K4):
                    ins = nc.tensor.transpose(MP[0:2 * E, k * P:(k + 1) * P], wcat[:, k, :], ident[:, :])
                ins.then_inc(mp_ready, 1)

            def transpose_output(L, b):
                pe.wait_ge(y_out, b + (NB * L + 1))
                if first(b) and L == 0:
                    pe.wait_ge(scl_ready, 1)
                else:
                    pe.wait_ge(me_free, me_no(L, b, 0))
                for k in range(K4):
                    ins = nc.tensor.transpose(ME[:, k * P:(k + 1) * P], YS[:, k * P:(k + 1) * P], ident[:, :])
                ins.then_inc(me_ready, 1)

            def transpose_messages(b):
                pe.wait_ge(e_normed, b + 1)
                pe.wait_ge(me_free, me_no(0, b, 1))
                for k in range(K4):
                    ins = nc.tensor.transpose(ME[:, k * P:(k + 1) * P], XLe[:, k * P:(k + 1) * P], ident[:, :])
                ins.then_inc(me_ready, 1)

            def messages(b):
                pe.wait_ge(me_free, me_no(0, b, 2))
                for k in range(K4):
                    ins = nc.tensor.matmul(ME[:, k * P:(k + 1) * P], xTe[:, k * P:(k + 1) * P], Wm[:, :],
                                           start=True, stop=True)
                ins.then_inc(me_ready, 1)

            def up(L, b, e, par):
                n = expert_no(L, b, e)
                s = e % 2
                if e == 0:
                    pe.wait_ge(xt_ready, b + (NB * L + 1))
                for c in range(HC):
                    pe.wait_ge(acted, n * 2 + (c + 1))
                    w = slice((e * HC + c) * P, (e * HC + c + 1) * P)
                    nc.tensor.matmul(HB[s][:, c, :], W1h[L][:, w], XTh[par][:, :], start=True, stop=False)
                    nc.tensor.matmul(HB[s][:, c, :], W1h[L][:, w], XTl[par][:, :], start=False, stop=False)
                    nc.tensor.matmul(HB[s][:, c, :], W1l[L][:, w], XTh[par][:, :], start=False,
                                     stop=True).then_inc(hid_ready, 1)

            def gate(L, b, e, par):
                if e == 0:
                    pe.wait_ge(mp_free, mp_no(L, b, 3) + 1)
                pe.wait_ge(gated, expert_no(L, b, e) + 2)
                nc.tensor.matmul(GB, sel[:, e * P:(e + 1) * P], wT[par][:, :], start=True,
                                 stop=True).then_inc(gb_ready, 1)

            def output_bias(L, b, par):
                if not (first(b) and L == 0):
                    pe.wait_ge(y_out, b + NB * L)
                nc.tensor.matmul(YB, b2h[L][:, :], wT[par][:, :], start=True, stop=False)
                nc.tensor.matmul(YB, b2l[L][:, :], wT[par][:, :], start=False, stop=False)

            def down(L, b, e):
                n = expert_no(L, b, e)
                pe.wait_ge(hi_ready, n + 1)
                for c in range(HC):
                    w = slice((e * HC + c) * D, (e * HC + c + 1) * D)
                    nc.tensor.matmul(YB, W2h[L][:, w], hhi[e % 2][:, c, :], start=False, stop=False)
                    nc.tensor.matmul(YB, W2l[L][:, w], hhi[e % 2][:, c, :], start=False, stop=False)
                for c in range(HC):
                    pe.wait_ge(lo_ready, n * 2 + (c + 1))
                    w = slice((e * HC + c) * D, (e * HC + c + 1) * D)
                    ins = nc.tensor.matmul(YB, W2h[L][:, w], hlo[e % NP][:, c, :],
                                           start=False, stop=(e == E - 1 and c == HC - 1))
                ins.then_inc(w2_done, 1)

            def experts(L):
                pe.wait_ge(evac_v[L], 2)
                graph_rows(L, 0)
                transpose_rows(L, 0)
                logits(L, 0)
                pe.wait_ge(evac_a[L], 4)
                pe.wait_ge(evac_v[L], 4)
                pe.wait_ge(split1, 2 * L + 2)
                up(L, 0, 0, 0)
                transpose_gates(L, 0)
                up(L, 0, 1, 0)
                gate(L, 0, 0, 0)
                up(L, 0, 2, 0)
                gate(L, 0, 1, 0)
                pe.wait_ge(split2, 2 * L + 2)

                def body(b, par):
                    ahead, behind = not last(b), not first(b)
                    for e in range(E):
                        if e == 0 and ahead:
                            graph_rows(L, b + 1)
                        nxt = ahead_of(b, e, par, 3)
                        if nxt:
                            up(L, *nxt)
                        nxt = ahead_of(b, e, par, 2)
                        if nxt:
                            gate(L, *nxt)
                        if e == 2 and ahead:
                            logits(L, b + 1)
                        if e == 6 and behind and L == 0:
                            transpose_messages(b - 1)
                        if e == 7 and behind and L == 0:
                            messages(b - 1)
                        if e == 0:
                            output_bias(L, b, par)
                        down(L, b, e)
                        if e == 1 and ahead:
                            transpose_rows(L, b + 1)
                        if e == 2 and behind:
                            transpose_output(L, b - 1)
                        if e == 4 and ahead:
                            transpose_gates(L, b + 1)

                blocks(pe, body)
                transpose_output(L, NB - 1)
                if L == 0:
                    transpose_messages(NB - 1)
                    messages(NB - 1)

            experts(0)
            pe.wait_ge(me_free, NB * M_END[0])
            pe.wait_ge(y_out, NB)
            pe.wait_ge(c_ready, NG)

            def graph2_cached(g, start=False):
                pe.wait_ge(msg_staged, g * G + 1)
                for b in range(NB):
                    ins = nc.tensor.matmul(bank[:, b, :], xs[0][:, :], C[:, bass.ds(g * N + b * BK, BK)],
                                           start=start, stop=False)
                ins.then_inc(prod2, 1)

            def graph2_streamed(k, u, s, stop=False):
                pe.wait_ge(msg_staged, k + 1)
                pe.wait_ge(f_ready, u + 1)
                product(1 - s % 2, ring[s], False, stop).then_inc(prod2, 1)

            def group(g, start=False):
                graph2_cached(g, start)
                for s in range(S2):
                    graph2_streamed(g * G + (1 + s), g * S2 + s, s)

            group(0, start=True)
            with pe.Fori(1, NG) as g:
                group(g)
            for s in range(2):
                pe.wait_ge(msg_staged, T - 1 + s)
                pe.wait_ge(f_ready, NG * S2 + s + 1)
                product(s, ring[s], False, s == 1).then_inc(prod2, 1)
            experts(1)


def kernel(x, adj, L0_gnn_kernel, L0_gnn_bias, L0_gnn_beta, L0_ffn_gamma, L0_ffn_beta, L0_ffn_Wr, L0_ffn_br,
           L0_ffn_W1, L0_ffn_b1, L0_ffn_W2, L0_ffn_b2, L1_gnn_W, L1_gnn_B, L1_ffn_Wg, L1_ffn_bg, L1_ffn_bias,
           L1_ffn_W1, L1_ffn_b1, L1_ffn_W2, L1_ffn_b2):
    import numpy as np
    import concourse.bacc as bacc
    from concourse import mybir as mb
    from concourse.bass_utils import run_bass_kernel_spmd

    N, D = np.shape(x)
    P = 128

    def rows(a):
        return np.asarray(a).reshape(N // P, P, D).transpose(1, 0, 2).reshape(P, -1)

    def up(w):
        return np.asarray(w).transpose(1, 0, 2).reshape(D, -1)

    def chunks(w):
        w = np.asarray(w)
        return w.reshape(w.shape[0], w.shape[1] // P, P, -1).transpose(2, 0, 1, 3).reshape(P, -1)

    ins = {
        "x_t": rows(x), "adj_t": np.asarray(adj).T, "kern0": L0_gnn_kernel, "bias0": L0_gnn_bias,
        "beta_t": np.asarray(L0_gnn_beta).reshape(N // P, P).T,
        "gamma": np.asarray(L0_ffn_gamma).reshape(D, 1), "beta_ln": np.asarray(L0_ffn_beta).reshape(D, 1),
        "wr": L0_ffn_Wr, "br": L0_ffn_br, "w1a": up(L0_ffn_W1), "b1a": chunks(L0_ffn_b1),
        "w2a": chunks(L0_ffn_W2), "b2a": L0_ffn_b2, "wm": L1_gnn_W, "bm": L1_gnn_B,
        "wg": L1_ffn_Wg, "bg": L1_ffn_bg, "gate_bias": L1_ffn_bias, "w1b": up(L1_ffn_W1),
        "b1b": chunks(L1_ffn_b1), "w2b": chunks(L1_ffn_W2), "b2b": L1_ffn_b2,
    }
    nc = bacc.Bacc("TRN2", target_bir_lowering=False, num_devices=1)
    arrays, args = {}, []
    for name, a in ins.items():
        a = np.ascontiguousarray(a)
        arrays[f"in_{name}"] = a
        args.append(nc.dram_tensor(f"in_{name}", a.shape, mb.dt.from_np(a.dtype), kind="ExternalInput").ap())
    args.append(nc.dram_tensor("out_x", (P, N), mb.dt.float32, kind="ExternalOutput").ap())
    gnn_moe_two_layers(nc, *args)
    r = run_bass_kernel_spmd(nc, [arrays], core_ids=[0])
    got = r.results[0]["out_x"]
    return got.reshape(P, N // P, D).transpose(1, 0, 2).reshape(N, D)
```

```python
import concourse.bass as bass
from concourse import mybir
from contextlib import ExitStack


def gnn_moe_two_layers(nc, x_t, adj_t, kern0, bias0, beta_t, gamma, beta_ln, wr, br, w1a, b1a, w2a, b2a,
                       wm, bm, wg, bg, gate_bias, w1b, b1b, w2b, b2b, out):
    F32, F32R, U32 = mybir.dt.float32, mybir.dt.float32r, mybir.dt.uint32
    ALU, ACT = mybir.AluOpType, mybir.ActivationFunctionType

    P = 128
    N = adj_t.shape[0]
    D = kern0.shape[0]
    E = wr.shape[1]
    H = w1a.shape[1] // E
    HC = H // P
    T = N // P
    BK = 512
    NB = N // BK
    K4 = BK // P
    EPS = 1e-5
    G = 6
    NG = 5
    S1 = 3
    S2 = 5
    NF = 3
    Q = N // 4
    RV = 192
    assert D == P and T == G * NG + 2 and NB == 8 and HC == 2 and E == 8
    CUTOFF = 1.0
    TINY = 1e-18

    ctx = ExitStack()
    with ctx:
        def sb(name, shape, dt=F32):
            return ctx.enter_context(nc.sbuf_tensor(name, shape, dt))

        def sem(name):
            return ctx.enter_context(nc.semaphore(name))

        TB = N * 4
        ARENA = (nc.sbuf_base + 31) // 32 * 32
        sb("arena", [P, (1 + NG + S2 + 1) * N + 8])

        def at(name, offset, shape, dt=F32):
            return nc.alloc_sbuf_tensor_at(name, shape, dt, offset=offset)

        R_C = ARENA + TB
        R_R = R_C + NG * TB
        R_A = R_R + S2 * TB
        X = at("X", ARENA, [P, N])
        o = R_A + TB // 8 * 5
        seed = at("seed", o, [2 * E, E * P])
        o += E * P * 4
        saved = at("saved", o, [P, P])
        xsh = [at(f"xsh{s}", o + (1 + s) * P * 4, [P, D], F32R) for s in range(2)]
        xsl = [at("xsl0", o + 3 * P * 4, [P, D], F32R), sb("xsl1", [P, D], F32R)]
        Klast = at("Klast", R_C + (NG - 1) * TB, [P, D])
        C = at("C", R_C, [P, NG * N])
        R3, R4 = R_R + 3 * TB, R_R + 4 * TB
        ring = [at(f"ring{s}", o, [P, N]) for s, o in enumerate((R_R + TB, R_A, R_R + 2 * TB, R3, R4))]
        AG = at("AG", R_R, [P, N])
        MSG = at("MSG", R_R, [P, N])
        ring1 = [at(f"ring1_{s}", o, [P, N]) for s, o in enumerate((R_R, R3, R4))]
        lo1 = [at(f"lo1_{s}", o, [P, N], F32R) for s, o in enumerate((R_R, R3, R4))]
        hi1 = at("hi1", R_A, [P, (NB - NF) * BK], F32R)
        PARTS = ((NF, NF + 2), (NF + 2, NB))
        BB = BK * 4
        o = R_R + 3 * TB
        NP = 4
        hid = [at(f"hid{s}", o + s * HC * BB, [P, HC, BK]) for s in range(NP)]
        hlo = [at(f"hlo{s}", o + s * HC * BB, [P, HC, BK], F32R) for s in range(NP)]
        hhi = [at(f"hhi{s}", R_A + s * HC * BB, [P, HC, BK], F32R) for s in range(2)]
        XTh = [at(f"XTh{s}", R_A + (4 + s) * BB, [P, BK], F32R) for s in range(2)]
        XTl = [at(f"XTl{s}", R_A + (6 + s) * BB, [P, BK], F32R) for s in range(2)]
        o = R_R + 4 * TB
        XL = at("XL", o, [P, BK])
        XLe = at("XLe", o + BB, [P, BK])
        YS = at("YS", o + 2 * BB, [P, BK])
        AGS = at("AGS", o + 3 * BB, [P, BK])
        xT = at("xT", o + 4 * BB, [P, BK])
        xTe = at("xTe", o + 5 * BB, [P, BK])
        wT = [at(f"wT{s}", o + (6 + s) * BB, [2 * E, BK], F32R) for s in range(2)]
        WBY = E * H * 4
        W1h, W1l, W1raw, W2h, W2l, W2raw = [], [], [], [], [], []
        for L, o in ((0, R_R + TB), (1, R_C)):
            for name, hi, lo, raw, k in (("W1", W1h, W1l, W1raw, 0), ("W2", W2h, W2l, W2raw, 2)):
                hi.append(at(f"{name}h{L}", o + k * WBY, [P, E * H], F32R))
                lo.append(at(f"{name}l{L}", o + (k + 1) * WBY, [P, E * H], F32R))
                raw.append(at(f"{name}raw{L}", o + (k + 1) * WBY, [P, E * H]))

        sel = sb("sel", [2 * E, E * P], F32R)
        ident = sb("ident", [P, P])
        Kw = sb("Kw", [P, D])
        Wm = sb("Wm", [P, D])
        Bm = sb("Bm", [P, D])
        B0 = sb("B0", [P, D])
        Wrt = [sb("Wr", [P, E]), sb("Wg", [P, E])]
        brt = [sb("br_bc", [P, E]), sb("bg_bc", [P, E])]
        gb_bc = sb("gb_bc", [P, E])
        gam = sb("gam", [P, 1])
        bet = sb("bet", [P, 1])
        b1t = [sb("b1_0", [P, E * HC]), sb("b1_1", [P, E * HC])]
        b2r = [sb("b2r0", [2 * E, D]), sb("b2r1", [2 * E, D])]
        b2h = [sb("b2h0", [2 * E, D], F32R), sb("b2h1", [2 * E, D], F32R)]
        b2l = [sb("b2l0", [2 * E, D], F32R), sb("b2l1", [2 * E, D], F32R)]
        btile = sb("btile", [P, T])
        scl = sb("scl", [P, T])
        scratch = sb("scratch", [P, 1])
        scratch_a = sb("scratch_a", [P, 8])
        tiny = sb("tiny", [P, 1])
        minus2 = sb("minus2", [P, 1])
        nhalf = sb("nhalf", [P, 8])
        euler = sb("euler", [P, K4])
        iota8 = sb("iota8", [P, E])
        xs = [sb(f"xs{s}", [P, D]) for s in range(3)]
        st = sb("st", [P, 8, 6])
        ste = sb("ste", [P, K4, 6])
        mve = sb("mve", [P, K4, 2])
        vee = sb("vee", [P, K4])
        rse = sb("rse", [P, K4])
        mv = sb("mv", [P, T, 2])
        ve = sb("ve", [P, T])
        rs = sb("rs", [P, T])
        lg = sb("lg", [P, K4, E])
        mx = sb("mx", [P, K4, 8])
        ix = sb("ix", [P, K4, 8], U32)
        ixf = sb("ixf", [P, 2, K4])
        dm = sb("dm", [P, K4])
        ex = sb("ex", [P, K4])
        sm = sb("sm", [P, K4])
        wp = sb("wp", [P, 2, K4])
        oh = sb("oh", [P, 2, K4, E])
        wf = sb("wf", [P, K4, E])
        wh = sb("wh", [P, K4, E], F32R)
        wcat = sb("wcat", [P, K4, 2 * E])

        bank = ctx.enter_context(nc.psum_tensor("bank", [P, 8, BK], F32))
        MP = bank[:, 0, :]
        ME = bank[:, 1, :]
        YB = bank[:, 2, :]
        GB = bank[:, 3, :]
        HB = [bank[:, 4 + 2 * s:6 + 2 * s, :] for s in range(2)]

        x_in = [sem(f"x_in{c}") for c in range(4)]
        beta_in = sem("beta_in")
        b0_in = sem("b0_in")
        params_in = sem("params_in")
        w_in = [sem("w_in0"), sem("w_in1")]
        w_in2 = sem("w_in2")
        loaded1 = [sem(f"loaded1_{s}") for s in range(S1)]
        loaded2 = [sem(f"loaded2_{s}") for s in range(S2)]
        consts = sem("consts")
        kw_ready = sem("kw_ready")
        smalls = sem("smalls")
        stats_done = sem("stats_done")
        aggr_done = sem("aggr_done")
        var_ready = sem("var_ready")
        rstd_ready = sem("rstd_ready")
        normed = sem("normed")
        e_stats = sem("e_stats")
        e_aggr = sem("e_aggr")
        e_var = sem("e_var")
        e_rstd = sem("e_rstd")
        e_normed = sem("e_normed")
        split1 = sem("split1")
        split2 = sem("split2")
        tile_ready = sem("tile_ready")
        xs_f = sem("xs_f")
        xs_h = sem("xs_h")
        xs_ready = sem("xs_ready")
        hi1_ready = sem("hi1_ready")
        lo1_ready = sem("lo1_ready")
        prod_a = sem("prod_a")
        prod1 = sem("prod1")
        loaded_c = sem("loaded_c")
        c_saved = sem("c_saved")
        c_restored = sem("c_restored")
        c_masked = sem("c_masked")
        c_log = sem("c_log")
        c_inverse = sem("c_inverse")
        c_square = sem("c_square")
        c_ready = sem("c_ready")
        biased = sem("biased")
        bank_done = [sem("bank_done0"), sem("bank_done1")]
        evac_a = [sem("evac_a0"), sem("evac_a1")]
        evac_v = [sem("evac_v0"), sem("evac_v1")]
        sums_ready = sem("sums_ready")
        scl_ready = sem("scl_ready")
        staged = sem("staged")
        mp_ready = sem("mp_ready")
        mp_free = sem("mp_free")
        me_ready = sem("me_ready")
        me_free = sem("me_free")
        xh_ready = sem("xh_ready")
        xt_ready = sem("xt_ready")
        route = sem("route")
        gap_ready = sem("gap_ready")
        exp_ready = sem("exp_ready")
        gates_ready = sem("gates_ready")
        hi_ready = sem("hi_ready")
        lo_ready = sem("lo_ready")
        hid_ready = sem("hid_ready")
        acted = sem("acted")
        gb_ready = sem("gb_ready")
        gated = sem("gated")
        w2_done = sem("w2_done")
        y_out = sem("y_out")
        masked = sem("masked")
        logged = sem("logged")
        inverse = sem("inverse")
        v_tiny = sem("v_tiny")
        v_inverse = sem("v_inverse")
        square = sem("square")
        f_ready = sem("f_ready")
        msg_staged = sem("msg_staged")
        prod2 = sem("prod2")
        stored = sem("stored")

        def tile(t):
            return bass.ds(t * P, P)

        def blk(b):
            return bass.ds(b * BK, BK)

        M_PRE, M_END = 4, (3, 1)
        N_FIRST = 4
        ROUTE = 10

        def mp_no(L, b, k):
            return b * M_PRE + (L * NB * M_PRE + k)

        def me_no(L, b, k):
            return b * M_END[L] + (L * NB * M_END[0] + k)

        def n_no(L, b):
            return b + L * NB

        def expert_no(L, b, e):
            return b * E + (L * NB * E + e)

        def blocks(eng, body):
            body(0, 0)
            with eng.Fori(0, (NB - 2) // 2) as g:
                body(g * 2 + 1, 1)
                body(g * 2 + 2, 0)
            body(NB - 1, 1)

        def ahead_of(b, e, par, steps):
            if e + steps < E:
                return b, e + steps, par
            return None if last(b) else (b + 1, e + steps - E, 1 - par)

        def first(b):
            return isinstance(b, int) and b == 0

        def last(b):
            return isinstance(b, int) and b == NB - 1

        def arrival1(g, k):
            return (None, g * 2 + 1, g * 2 + 2, g + 1, g * 2 + 2, g * 2 + 3)[k]

        params = [(Kw[:, :], kern0), (Klast[:, :], kern0[D - 1:D, :].partition_broadcast(P)), (Wm[:, :], wm), (Bm[:, :], bm.partition_broadcast(P)),
                  (Wrt[0][:, :], wr), (Wrt[1][:, :], wg),
                  (brt[0][:, :], br.partition_broadcast(P)), (brt[1][:, :], bg.partition_broadcast(P)),
                  (gb_bc[:, :], gate_bias.partition_broadcast(P)), (gam[:, :], gamma), (bet[:, :], beta_ln),
                  (b1t[0][:, :], b1a), (b1t[1][:, :], b1b)]
        for L, b2 in ((0, b2a), (1, b2b)):
            params += [(b2r[L][0:E, :], b2), (b2r[L][E:2 * E, :], b2)]
        PARAMS = len(params)

        block = ctx.enter_context(nc.Block())

        @block.sync
        def _(sp):
            def load_x(c):
                sp.dma_start(X[:, c * 8 * P:(c + 1) * 8 * P], x_t[:, c * 8 * P:(c + 1) * 8 * P]).then_inc(x_in[c], 16)

            def load1(t, s):
                sp.wait_ge(prod1, t + 1)
                sp.dma_start(ring1[s][:, :], adj_t[tile(t), :]).then_inc(loaded1[s], 16)

            load_x(0)
            load1(0, 0)
            sp.dma_start(btile[:, :], beta_t).then_inc(beta_in, 16)
            sp.dma_start(B0[:, :], bias0.partition_broadcast(P)).then_inc(b0_in, 16)
            for c in range(1, 4):
                load_x(c)

            def group_loads1(g):
                sp.dma_start(C[:, bass.ds(g * N, N)], adj_t[tile(g * G + 1), :]).then_inc(loaded_c, 16)
                for k in range(1, G):
                    load1(g * G + (1 + k), (1 + k) % S1)
                    if first(g) and k == 2:
                        for dst, src in params:
                            sp.dma_start(dst, src).then_inc(params_in, 16)

            group_loads1(0)
            with sp.Fori(1, NG) as g:
                sp.wait_ge(prod1, g * G + (1 + 1))
                group_loads1(g)
            load1(T - 1, (T - 1) % S1)
            sp.dma_start(W1raw[0][:, :], w1a).then_inc(w_in[0], 16)
            sp.dma_start(W2raw[0][:, :], w2a).then_inc(w_in2, 16)

            def load2(t, s):
                sp.dma_start(ring[s][:, :], adj_t[tile(t), :]).then_inc(loaded2[s], 16)

            sp.wait_ge(hid_ready, HC * E * NB)
            load2(2, 0)
            sp.wait_ge(w2_done, NP + E * NB)
            load2(3, 1)
            load2(4, 2)
            load2(5, 3)
            sp.wait_ge(me_free, NB * M_END[0])
            load2(6, 4)
            with sp.Fori(1, NG) as g:
                for k in range(1, G):
                    sp.wait_ge(prod2, g * G + (k - G + (2 if k == 1 else 3)))
                    load2(g * G + (1 + k), k - 1)
            sp.dma_start(W1raw[1][:, :], w1b).then_inc(w_in[1], 16)
            sp.dma_start(W2raw[1][:, :], w2b).then_inc(w_in[1], 16)
            for s, t in ((0, 0), (1, T - 1)):
                sp.wait_ge(prod2, (NG - 1) * G + (s + 1) + 3)
                load2(t, s)

            def store(b):
                sp.wait_ge(me_free, me_no(1, b, 0) + 1)
                sp.dma_start(out[:, blk(b)], X[:, blk(b)]).then_inc(stored, 16)

            with sp.Fori(0, NB - 1) as b:
                store(b)
            store(NB - 1)
            sp.wait_ge(stored, 16 * NB)

        @block.gpsimd
        def _(pool):
            pool.memset(ident[:, :], 0.0).then_inc(consts, 1)
            pool.memset(seed[:, :], 0.0).then_inc(consts, 1)
            for s in range(2):
                pool.memset(xs[s][:, D - 1:D], 1.0).then_inc(consts, 1)
            pool.memset(tiny[:, :], TINY).then_inc(consts, 1)
            pool.memset(minus2[:, :], -2.0).then_inc(consts, 1)
            pool.memset(nhalf[:, :], -0.5).then_inc(consts, 1)
            pool.memset(euler[:, :], 2.718281828459045).then_inc(consts, 1)
            pool.iota(iota8[:, :], [[1, E]], base=0, channel_multiplier=0,
                      allow_small_or_imprecise_dtypes=True).then_inc(consts, 1)
            pool.wait_ge(consts, 9)
            pool.affine_select(out=ident[:, :], in_=ident[:, :], compare_op=ALU.not_equal, fill=1.0, base=0,
                               pattern=[[-1, P]], channel_multiplier=1).then_inc(consts, 1)
            v = seed[:, :].rearrange("p (e q) -> p e q", q=P)
            for r in range(2):
                if r:
                    pool.wait_ge(consts, 11)
                pool.affine_select(out=v, in_=v, compare_op=ALU.not_equal, fill=1.0, base=-E * r,
                                   pattern=[[-1, E], [0, P]], channel_multiplier=1).then_inc(consts, 1)

            def first_powers(c):
                pool.wait_ge(var_ready, c + 1)
                pool.tensor_tensor(rs[:, 8 * c:8 * c + 8], ve[:, 8 * c:8 * c + 8], nhalf[:, :],
                                   ALU.pow).then_inc(rstd_ready, 1)

            def split_low(L, hi, lo, raw, done, halves=(0, 1)):
                pool.wait_ge(done, 3 * L + 1)
                for h in halves:
                    c = slice(h * E * H // 2, (h + 1) * E * H // 2)
                    pool.tensor_tensor(lo[:, c], raw[:, c], hi[:, c].bitcast(F32), ALU.subtract).then_inc(done, 1)

            def stationary(t, s):
                pool.wait_ge(xs_f, t + 1)
                pool.wait_ge(prod1, t + 2)
                pool.tensor_tensor(X[:, tile(t)], X[:, tile(t)], B0[:, :], ALU.add).then_inc(biased, 1)
                pool.tensor_copy(xsh[s][:, :], xs[s][:, :]).then_inc(xs_h, 1)
                pool.wait_ge(xs_h, t + 1)
                pool.tensor_tensor(xsl[s][:, :], xs[s][:, :], xsh[s][:, :].bitcast(F32), ALU.subtract).then_inc(xs_ready, 1)

            first_powers(0)
            pool.wait_ge(b0_in, 16)
            stationary(0, 0)
            first_powers(1)
            first_powers(2)
            for k in range(G):
                stationary(1 + k, (1 + k) % 2)
                if k == 3:
                    first_powers(3)
            with pool.Fori(1, NG) as g:
                for k in range(G):
                    stationary(g * G + (1 + k), (1 + k) % 2)
            stationary(T - 1, (T - 1) % 2)
            split_low(0, W1h[0], W1l[0], W1raw[0], split1, (0,))

            def power(n):
                pool.wait_ge(var_ready, n + (N_FIRST + 1))
                pool.tensor_tensor(rs[:, 0:K4], ve[:, 0:K4], nhalf[:, 0:K4], ALU.pow).then_inc(rstd_ready, 1)

            def stage(L, b):
                pool.tensor_copy(AGS[:, :], AG[:, blk(b)]).then_inc(staged, 1)

            def end(b):
                pool.wait_ge(e_var, b + 1)
                pool.tensor_tensor(rse[:, :], vee[:, :], nhalf[:, 0:K4], ALU.pow).then_inc(e_rstd, 1)

            def gate_exp(L, b):
                pool.wait_ge(gap_ready, b + (NB * L + 1))
                pool.tensor_tensor(ex[:, :], euler[:, :], dm[:, :], ALU.pow).then_inc(exp_ready, 1)

            def low_hidden(L, b, e):
                n = expert_no(L, b, e)
                pool.wait_ge(hi_ready, n + 1)
                for c in range(HC):
                    pool.tensor_tensor(hlo[e % NP][:, c, :], hid[e % NP][:, c, :], hhi[e % 2][:, c, :].bitcast(F32),
                                       ALU.subtract).then_inc(lo_ready, 1)

            def experts(L):
                power(n_no(L, 0))
                if L == 0:
                    split_low(0, W1h[0], W1l[0], W1raw[0], split1, (1,))
                gate_exp(L, 0)
                if L == 0:
                    split_low(0, W2h[0], W2l[0], W2raw[0], split2)
                pool.wait_ge(evac_a[L], 3)
                pool.wait_ge(evac_v[L], 4)
                pool.wait_ge(mp_ready, mp_no(L, 0, 0) + 1)
                stage(L, 1)
                for e in range(2):
                    low_hidden(L, 0, e)

                def body(b, par):
                    for e in range(E):
                        if e == 0 and not last(b):
                            power(n_no(L, b + 1))
                        if e == 3 and not last(b):
                            gate_exp(L, b + 1)
                        nxt = ahead_of(b, e, par, 2)
                        if nxt:
                            low_hidden(L, *nxt[:2])
                        if e == 1 and L == 0 and not first(b):
                            end(b - 1)
                        if e == 5 and not last(b) and not (isinstance(b, int) and b == NB - 2):
                            pool.wait_ge(mp_ready, mp_no(L, b + 1, 0) + 1)
                            stage(L, b + 2)

                body(0, 0)
                with pool.Fori(0, (NB - 4) // 2) as g:
                    body(g * 2 + 1, 1)
                    body(g * 2 + 2, 0)
                body(NB - 3, 1)
                body(NB - 2, 0)
                body(NB - 1, 1)
                if L == 0:
                    end(NB - 1)

            experts(0)

            def message(k, t, s):
                pool.wait_ge(prod2, k + 1)
                pool.tensor_copy(xs[s][:, :], MSG[:, tile(t)]).then_inc(msg_staged, 1)

            pool.wait_ge(me_free, NB * M_END[0])
            with pool.Fori(0, NG) as g:
                for k in range(G):
                    message(g * G + k, g * G + (1 + k), k % 3)
            message(T - 2, 0, 0)
            message(T - 1, T - 1, 1)
            pool.wait_ge(w_in[1], 32)
            pool.tensor_copy(W1h[1][:, :], W1raw[1][:, :]).then_inc(split1, 1)
            split_low(1, W1h[1], W1l[1], W1raw[1], split1)
            experts(1)

        @block.vector
        def _(dve):
            def settle():
                nc.vector.memset(scratch[:, :], 0.0)

            def norm_stats(n, src, factor, eps):
                settle()
                for k in range(K4):
                    ins = nc.vector.bn_stats(st[:, k, :], src(k))
                ins.then_inc(stats_done, 1)
                dve.wait_ge(stats_done, n + (N_FIRST + 1))
                settle()
                for k in range(K4):
                    ins = nc.vector.bn_aggr(mv[:, k, :], st[:, k, :])
                ins.then_inc(aggr_done, 1)
                dve.wait_ge(aggr_done, n + (N_FIRST + 1))
                nc.vector.tensor_scalar(ve[:, 0:K4], mv[:, 0:K4, 1], factor, eps, ALU.mult, ALU.add).then_inc(var_ready, 1)

            def normalise(n, src):
                dve.wait_ge(rstd_ready, n + (N_FIRST + 1))
                for k in range(K4):
                    ins = nc.vector.tensor_scalar(XL[:, k * P:(k + 1) * P], src(k), mv[:, k, 0:1], rs[:, k:k + 1],
                                                  ALU.subtract, ALU.mult)
                ins.then_inc(normed, 1)

            def end_stats(b):
                settle()
                for k in range(K4):
                    ins = nc.vector.bn_stats(ste[:, k, :], X[:, tile(b * K4 + k)])
                ins.then_inc(e_stats, 1)
                dve.wait_ge(e_stats, b + 1)
                settle()
                for k in range(K4):
                    ins = nc.vector.bn_aggr(mve[:, k, :], ste[:, k, :])
                ins.then_inc(e_aggr, 1)
                dve.wait_ge(e_aggr, b + 1)
                nc.vector.tensor_scalar(vee[:, :], mve[:, :, 1], EPS, None, ALU.add).then_inc(e_var, 1)

            def end_normalise(b):
                dve.wait_ge(e_rstd, b + 1)
                for k in range(K4):
                    ins = nc.vector.tensor_scalar(XLe[:, k * P:(k + 1) * P], X[:, tile(b * K4 + k)], mve[:, k, 0:1],
                                                  rse[:, k:k + 1], ALU.subtract, ALU.mult)
                ins.then_inc(e_normed, 1)

            def X_rows(b):
                return lambda k: X[:, tile(b * K4 + k)]

            dve.sem_inc(gated, 2)

            def evacuate(L, banks):
                for b in banks:
                    dve.wait_ge(bank_done[L], b + 1)
                    nc.vector.tensor_copy(AG[:, b * BK:(b + 1) * BK], bank[:, b, :]).then_inc(evac_v[L], 1)

            def first_stats(c):
                dve.wait_ge(x_in[c], 16)
                for k in range(8):
                    t = 8 * c + k
                    ins = nc.vector.bn_stats(st[:, k, :], X[:, t * P:(t + 1) * P])
                ins.then_inc(stats_done, 1)
                dve.wait_ge(stats_done, c + 1)
                for k in range(8):
                    ins = nc.vector.bn_aggr(mv[:, 8 * c + k, :], st[:, k, :])
                ins.then_inc(aggr_done, 1)
                dve.wait_ge(aggr_done, c + 1)
                nc.vector.tensor_scalar(ve[:, 8 * c:8 * c + 8], mv[:, 8 * c:8 * c + 8, 1], EPS, None,
                                        ALU.add).then_inc(var_ready, 1)

            def small_operands():
                dve.wait_ge(params_in, PARAMS * 16)
                for L in range(2):
                    nc.vector.tensor_copy(b2h[L][:, :], b2r[L][:, :]).then_inc(smalls, 1)
                nc.vector.tensor_tensor(Kw[:, :], Kw[:, :], Klast[:, :], ALU.subtract).then_inc(kw_ready, 1)
                nc.vector.tensor_tensor(brt[1][:, :], brt[1][:, :], gb_bc[:, :], ALU.add).then_inc(smalls, 1)
                dve.wait_ge(smalls, 3)
                for L in range(2):
                    nc.vector.tensor_tensor(b2l[L][:, :], b2r[L][:, :], b2h[L][:, :].bitcast(F32),
                                            ALU.subtract).then_inc(smalls, 1)
                dve.wait_ge(consts, 12)
                nc.vector.tensor_copy(sel[:, :], seed[:, :]).then_inc(smalls, 1)

            first_stats(0)
            dve.wait_ge(beta_in, 16)
            dve.wait_ge(consts, 10)
            dve.wait_ge(rstd_ready, 1)

            def prepare(t, s, xslot, arrivals, cached=None):
                if cached is None:
                    dve.wait_ge(loaded1[s], arrivals * 16)
                    block = ring1[s][:, tile(t)]
                else:
                    dve.wait_ge(loaded_c, cached * 16 + 16)
                    block = C[:, bass.ds(cached * N + t * P, P)]
                    nc.vector.tensor_copy(saved[:, :], block).then_inc(c_saved, 1)
                dve.wait_ge(prod1, t + 2)
                nc.vector.tensor_scalar(xs[xslot][:, 0:D - 1], X[:, bass.ds(t * P, D - 1)], mv[:, bass.ds(t, 1), 0],
                                        rs[:, bass.ds(t, 1)], ALU.subtract, ALU.mult).then_inc(xs_f, 1)
                if cached is not None:
                    dve.wait_ge(c_saved, cached + 1)
                nc.vector.scalar_tensor_tensor(block, ident[:, :], btile[:, bass.ds(t, 1)],
                                               block, ALU.mult, ALU.add).then_inc(tile_ready, 1)

            def low_tile(t, s, part, cached=None):
                c = slice(PARTS[part][0] * BK, PARTS[part][1] * BK)
                h = slice(c.start - NF * BK, c.stop - NF * BK)
                src = ring1[s][:, c] if cached is None else C[:, bass.ds(cached * N + c.start, c.stop - c.start)]
                dve.wait_ge(hi1_ready, t * 2 + (part + 1))
                nc.vector.tensor_tensor(lo1[s][:, c], src, hi1[:, h].bitcast(F32), ALU.subtract).then_inc(lo1_ready, 1)

            def cached_piece(g, k, half):
                if k == 1 and half == 0:
                    dve.wait_ge(prod1, g * G + (1 + 1 + S1))
                    nc.vector.tensor_copy(C[:, bass.ds(g * N + (g * G + 1) * P, P)], saved[:, :]).then_inc(c_restored, 1)
                    dve.wait_ge(c_restored, g + 1)
                if k in (1, 2):
                    v = C[:, bass.ds(g * N + (2 * (k - 1) + half) * Q, Q)]
                    nc.vector.scalar_tensor_tensor(v, v, CUTOFF, v, ALU.is_lt, ALU.mult).then_inc(c_masked, 1)
                if k in (4, 5):
                    if half == 0:
                        dve.wait_ge(c_inverse, g * 2 + (k - 3))
                    v = C[:, bass.ds(g * N + (2 * (k - 4) + half) * Q, Q)]
                    nc.vector.scalar_tensor_tensor(v, v, 2.0, v, ALU.subtract, ALU.mult).then_inc(c_square, 1)

            prepare(0, 0, 0, 1)
            low_tile(0, 0, 0)
            low_tile(0, 0, 1)
            first_stats(1)
            first_stats(2)
            prepare(1, 1, 1, None, 0)

            def group(g):
                for k in range(G):
                    t = 1 + k
                    cached = g if k == 0 else None
                    low_tile(g * G + t, t % S1, 0, cached)
                    low_tile(g * G + t, t % S1, 1, cached)
                    cached_piece(g, k, 0)
                    if first(g) and k == 5:
                        dve.wait_ge(rstd_ready, N_FIRST)
                    if k < G - 1:
                        prepare(g * G + (t + 1), (t + 1) % S1, (t + 1) % 2, arrival1(g, k + 1))
                    elif isinstance(g, int) and g == NG - 1:
                        prepare(T - 1, (T - 1) % S1, (T - 1) % 2, NG + 1)
                    else:
                        prepare(g * G + (t + 1), (t + 1) % S1, (t + 1) % 2, None, g + 1)
                    cached_piece(g, k, 1)
                    if first(g) and k == 3:
                        first_stats(3)
                    if first(g) and k == 5:
                        small_operands()

            group(0)
            with dve.Fori(1, NG - 1) as g:
                group(g)
            group(NG - 1)
            low_tile(T - 1, (T - 1) % S1, 0)
            low_tile(T - 1, (T - 1) % S1, 1)
            v = ME.rearrange("p (k d) -> p k d", d=D)
            dve.wait_ge(sums_ready, 1)
            nc.vector.reciprocal(scl[:, 0:K4], v[:, :, D - 1]).then_inc(scl_ready, 1)
            dve.wait_ge(scl_ready, 1)
            dve.wait_ge(biased, T)

            def gate_hidden(L, b, e):
                n = expert_no(L, b, e)
                dve.wait_ge(acted, n * 2 + 6)
                dve.wait_ge(gb_ready, n + 1)
                h = hid[e % NP]
                nc.vector.tensor_tensor(h[:, :, :], h[:, :, :],
                                        GB.unsqueeze(1).to_broadcast([P, HC, BK]), ALU.mult).then_inc(gated, 1)

            def add_graph(L, b):
                u = mp_no(L, b, 0)
                dve.wait_ge(mp_ready, u + 1)
                if L == 0:
                    for k in range(K4):
                        t = b * K4 + k
                        ins = nc.vector.scalar_tensor_tensor(X[:, tile(t)], MP[:, k * P:(k + 1) * P],
                                                             scl[:, bass.ds(t, 1)], X[:, tile(t)], ALU.mult, ALU.add)
                else:
                    ins = nc.vector.tensor_tensor(X[:, blk(b)], MP, X[:, blk(b)], ALU.add)
                ins.then_inc(mp_free, 1)
                dve.wait_ge(mp_free, u + 1)
                if L == 0:
                    norm_stats(n_no(L, b), X_rows(b), 1.0 + EPS, EPS * EPS)
                else:
                    norm_stats(n_no(L, b), X_rows(b), 1.0, EPS)

            def low_part(L, b, par):
                dve.wait_ge(xh_ready, b + (NB * L + 1))
                nc.vector.tensor_tensor(XTl[par][:, :], xT[:, :], XTh[par][:, :].bitcast(F32),
                                        ALU.subtract).then_inc(xt_ready, 1)

            def route_first(L, b):
                u = mp_no(L, b, 2)
                r = b * ROUTE + NB * L * ROUTE
                dve.wait_ge(mp_ready, u + 1)
                nc.vector.tensor_tensor(lg[:, :, :], MP[:, 0:K4 * E].rearrange("p (k e) -> p k e", e=E),
                                        brt[L][:, :].unsqueeze(1).to_broadcast([P, K4, E]), ALU.add).then_inc(mp_free, 1)
                dve.wait_ge(mp_free, u + 1)
                settle()
                for k in range(K4):
                    ins = nc.vector.max(mx[:, k, :], lg[:, k, :])
                ins.then_inc(route, 1)
                dve.wait_ge(route, r + 1)
                nc.vector.tensor_tensor(dm[:, :], mx[:, :, 1], mx[:, :, 0], ALU.subtract).then_inc(gap_ready, 1)
                for k in range(K4):
                    ins = nc.vector.max_index(ix[:, k, :], mx[:, k, :], lg[:, k, :])
                ins.then_inc(route, 1)
                dve.wait_ge(route, r + 2)
                nc.vector.tensor_copy(ixf[:, :, :], ix[:, :, 0:2].rearrange("p k j -> p j k")).then_inc(route, 1)
                dve.wait_ge(route, r + 3)
                for j in range(2):
                    ins = nc.vector.tensor_tensor(oh[:, j, :, :], iota8[:, :].unsqueeze(1).to_broadcast([P, K4, E]),
                                                  ixf[:, j, :].unsqueeze(2).to_broadcast([P, K4, E]), ALU.is_equal)
                ins.then_inc(route, 1)

            def route_second(L, b):
                r = b * ROUTE + NB * L * ROUTE
                dve.wait_ge(exp_ready, b + (NB * L + 1))
                nc.vector.tensor_scalar(sm[:, :], ex[:, :], 1.0, None, ALU.add).then_inc(route, 1)
                dve.wait_ge(route, r + 5)
                nc.vector.reciprocal(wp[:, 0, :], sm[:, :]).then_inc(route, 1)
                dve.wait_ge(route, r + 6)
                nc.vector.tensor_tensor(wp[:, 1, :], wp[:, 0, :], ex[:, :], ALU.mult).then_inc(route, 1)
                dve.wait_ge(route, r + 7)
                v = oh[:, :, :, :].rearrange("p j k e -> p (j k) e")
                w = wp[:, :, :].rearrange("p j k -> p (j k)")
                nc.vector.tensor_tensor(v, v, w.unsqueeze(2).to_broadcast([P, 2 * K4, E]), ALU.mult).then_inc(route, 1)
                dve.wait_ge(route, r + 8)
                nc.vector.tensor_tensor(wf[:, :, :], oh[:, 0, :, :], oh[:, 1, :, :], ALU.add).then_inc(route, 1)
                dve.wait_ge(route, r + 9)
                nc.vector.tensor_copy(wh[:, :, :], wf[:, :, :]).then_inc(route, 1)
                dve.wait_ge(route, r + 10)
                nc.vector.tensor_copy(wcat[:, :, 0:E], wh[:, :, :].bitcast(F32))
                nc.vector.tensor_tensor(wcat[:, :, E:2 * E], wf[:, :, :], wh[:, :, :].bitcast(F32),
                                        ALU.subtract).then_inc(gates_ready, 1)

            def add_experts(L, b):
                u = me_no(L, b, 0)
                dve.wait_ge(me_ready, u + 1)
                nc.vector.tensor_tensor(X[:, blk(b)], ME, X[:, blk(b)], ALU.add).then_inc(me_free, 1)
                if L == 0:
                    dve.wait_ge(me_free, u + 1)
                    end_stats(b)

            def message_out(b):
                dve.wait_ge(me_ready, me_no(0, b, 2) + 1)
                nc.vector.tensor_tensor(MSG[:, blk(b)].rearrange("p (k d) -> p k d", d=D),
                                        ME.rearrange("p (k d) -> p k d", d=D),
                                        Bm[:, :].unsqueeze(1).to_broadcast([P, K4, D]), ALU.add).then_inc(me_free, 1)

            def experts(L):
                add_graph(L, 0)
                evacuate(L, (4, 5))
                normalise(n_no(L, 0), X_rows(0))
                evacuate(L, (6, 7))
                low_part(L, 0, 0)
                route_first(L, 0)
                route_second(L, 0)
                if L == 0:
                    dve.wait_ge(sums_ready, 2)
                    v = bank[:, 1:, :].rearrange("p b (k d) -> p b k d", d=D)
                    nc.vector.reciprocal(scl[:, K4:T].rearrange("p (b k) -> p b k", k=K4),
                                         v[:, :, :, D - 1]).then_inc(scl_ready, 1)
                for e in range(2):
                    gate_hidden(L, 0, e)

                def body(b, par):
                    ahead, behind = not last(b), not first(b)
                    for e in range(E):
                        if e == 0 and ahead:
                            add_graph(L, b + 1)
                        if e == 1 and ahead:
                            normalise(n_no(L, b + 1), X_rows(b + 1))
                        if e == 3 and ahead:
                            route_first(L, b + 1)
                        nxt = ahead_of(b, e, par, 2)
                        if nxt:
                            gate_hidden(L, *nxt[:2])
                        if e == 1 and behind:
                            add_experts(L, b - 1)
                        if e == 2 and ahead:
                            low_part(L, b + 1, 1 - par)
                        if e == 4 and ahead:
                            route_second(L, b + 1)
                        if e == 3 and behind and L == 0:
                            end_normalise(b - 1)
                        if e == 7 and behind and L == 0:
                            message_out(b - 1)

                blocks(dve, body)
                if L == 0:
                    mask(0, 0, 1)
                add_experts(L, NB - 1)
                if L == 0:
                    end_normalise(NB - 1)
                    mask(1, 1, 1)
                    message_out(NB - 1)

            def mask(u, s, arrivals):
                dve.wait_ge(loaded2[s], arrivals * 16)
                nc.vector.scalar_tensor_tensor(ring[s][:, :], ring[s][:, :], CUTOFF, ring[s][:, :],
                                               ALU.is_lt, ALU.mult).then_inc(masked, 1)
                v = ring[s][:, 0:RV]
                dve.wait_ge(masked, u + 1)
                nc.vector.tensor_scalar(v, v, TINY, None, ALU.add).then_inc(v_tiny, 1)
                dve.wait_ge(v_tiny, u + 1)
                nc.vector.reciprocal(v, v).then_inc(v_inverse, 1)

            experts(0)

            def square_streamed(u, s):
                dve.wait_ge(inverse, u + 1)
                dve.wait_ge(v_inverse, u + 1)
                nc.vector.scalar_tensor_tensor(ring[s][:, :], ring[s][:, :], 2.0, ring[s][:, :],
                                               ALU.subtract, ALU.mult).then_inc(square, 1)

            def stream(g):
                for s in range(S2):
                    if not (first(g) and s == 0):
                        square_streamed(g * S2 + s, s)
                    mask(g * S2 + (s + 2), (s + 2) % S2, g + (1 + (s + 2) // S2))
                    if first(g) and s == 0:
                        square_streamed(0, 0)

            stream(0)
            with dve.Fori(1, NG) as g:
                stream(g)
            for s in range(2):
                square_streamed(NG * S2 + s, s)
            dve.wait_ge(w_in[1], 32)
            nc.vector.tensor_copy(W2h[1][:, :], W2raw[1][:, :]).then_inc(split2, 1)
            dve.wait_ge(split2, 4)
            nc.vector.tensor_tensor(W2l[1][:, :], W2raw[1][:, :], W2h[1][:, :].bitcast(F32),
                                    ALU.subtract).then_inc(split2, 2)
            experts(1)

        @block.scalar
        def _(act):
            act.sem_inc(acted, 4)
            act.preload_act_table_set("natural_log_exp_and_others")
            act.wait_ge(consts, 9)

            def take_wait(i):
                nc.scalar.activation(scratch_a[:, i:i + 1], minus2[:, :], ACT.Copy)

            def high_tile(t, s, cached=None):
                act.wait_ge(tile_ready, t + 1)
                for part, (b0, b1) in enumerate(PARTS):
                    if part == 0:
                        act.wait_ge(prod_a, t + 1)
                    else:
                        act.wait_ge(prod1, t + S1)
                    n = (b1 - b0) * BK
                    if cached is None:
                        src = ring1[s][:, b0 * BK:b1 * BK]
                    else:
                        take_wait(part)
                        src = C[:, bass.ds(cached * N + b0 * BK, n)]
                    nc.scalar.activation(hi1[:, (b0 - NF) * BK:(b1 - NF) * BK], src, ACT.Copy).then_inc(hi1_ready, 1)

            def cached_log(g, h):
                act.wait_ge(c_masked, g * 4 + (2 * h + 2))
                take_wait(2 + h)
                v = C[:, bass.ds(g * N + h * 2 * Q, 2 * Q)]
                nc.scalar.activation(v, v, ACT.Ln, bias=tiny[:, :]).then_inc(c_log, 1)

            def cached_inverse(g, h):
                act.wait_ge(c_log, g * 2 + (h + 1))
                take_wait(4 + h)
                v = C[:, bass.ds(g * N + h * 2 * Q, 2 * Q)]
                nc.scalar.activation(v, v, ACT.Exp, scale=-1.0).then_inc(c_inverse, 1)

            def cached_exp(g, h):
                act.wait_ge(c_square, g * 4 + (2 * h + 2))
                take_wait(6 + h)
                v = C[:, bass.ds(g * N + h * 2 * Q, 2 * Q)]
                nc.scalar.activation(v, v, ACT.Exp, scale=-2.0, bias=minus2[:, :]).then_inc(c_ready, 1)

            def group(g):
                for k in range(G):
                    high_tile(g * G + (1 + k), (1 + k) % S1, g if k == 0 else None)
                    if k == 0 and not first(g):
                        cached_exp(g - 1, 1)
                    if k == 2:
                        cached_log(g, 0)
                    if k == 3:
                        cached_log(g, 1)
                        cached_inverse(g, 0)
                    if k == 4:
                        cached_inverse(g, 1)
                    if k == 5:
                        cached_exp(g, 0)

            high_tile(0, 0)
            group(0)
            with act.Fori(1, NG) as g:
                group(g)
            high_tile(T - 1, (T - 1) % S1)
            cached_exp(NG - 1, 1)

            def evacuate(L):
                act.wait_ge(bank_done[L], 1)
                nc.scalar.activation(AGS[:, :], bank[:, 0, :], ACT.Copy).then_inc(staged, 1)
                for b in range(1, 4):
                    act.wait_ge(bank_done[L], b + 1)
                    nc.scalar.activation(AG[:, b * BK:(b + 1) * BK], bank[:, b, :], ACT.Copy).then_inc(evac_a[L], 1)
                    if L == 0 and b == 1:
                        act.wait_ge(w_in[0], 16)
                        nc.scalar.activation(W1h[0][:, :], W1raw[0][:, :], ACT.Copy).then_inc(split1, 1)
                if L == 0:
                    act.wait_ge(w_in2, 16)
                    nc.scalar.activation(W2h[0][:, :], W2raw[0][:, :], ACT.Copy).then_inc(split2, 1)

            evacuate(0)
            act.preload_act_table_set("gelu_and_others")

            def hidden(L, b, e):
                n = expert_no(L, b, e)
                act.wait_ge(w2_done, n + 1)
                for c in range(HC):
                    act.wait_ge(hid_ready, n * 2 + (c + 1))
                    nc.scalar.activation(hid[e % NP][:, c, :], HB[e % 2][:, c, :], ACT.Gelu if L == 0 else ACT.Relu,
                                         bias=b1t[L][:, e * HC + c:e * HC + c + 1]).then_inc(acted, 1)

            def high_hidden(L, b, e):
                n = expert_no(L, b, e)
                act.wait_ge(gated, n + 3)
                act.wait_ge(w2_done, n + 3)
                nc.scalar.activation(hhi[e % 2][:, :, :], hid[e % NP][:, :, :], ACT.Copy).then_inc(hi_ready, 1)

            def transposed_rows(L, b, par):
                u = mp_no(L, b, 1)
                act.wait_ge(mp_ready, u + 1)
                if L == 0:
                    nc.scalar.activation(xT[:, :], MP, ACT.Identity, scale=gam[:, :], bias=bet[:, :]).then_inc(mp_free, 1)
                else:
                    nc.scalar.activation(xT[:, :], MP, ACT.Copy).then_inc(mp_free, 1)
                act.wait_ge(mp_free, u + 1)
                nc.scalar.activation(XTh[par][:, :], xT[:, :], ACT.Copy).then_inc(xh_ready, 1)

            def transposed_gates(L, b, par):
                act.wait_ge(mp_ready, mp_no(L, b, 3) + 1)
                nc.scalar.activation(wT[par][:, :], MP[0:2 * E, :], ACT.Copy).then_inc(mp_free, 1)

            def message_rows(b):
                act.wait_ge(me_ready, me_no(0, b, 1) + 1)
                nc.scalar.activation(xTe[:, :], ME, ACT.Copy).then_inc(me_free, 1)

            def invert_first(u, s):
                act.wait_ge(masked, u + 1)
                nc.scalar.activation(ring[s][:, RV:N], ring[s][:, RV:N], ACT.Ln, bias=tiny[:, :]).then_inc(logged, 1)

            def invert_second(u, s):
                act.wait_ge(logged, u + 1)
                nc.scalar.activation(ring[s][:, RV:N], ring[s][:, RV:N], ACT.Exp, scale=-1.0).then_inc(inverse, 1)

            def experts(L):
                transposed_rows(L, 0, 0)
                transposed_gates(L, 0, 0)
                hidden(L, 0, 0)
                hidden(L, 0, 1)
                high_hidden(L, 0, 0)
                hidden(L, 0, 2)
                high_hidden(L, 0, 1)

                def body(b, par):
                    ahead, behind = not last(b), not first(b)
                    for e in range(E):
                        nxt = ahead_of(b, e, par, 3)
                        if nxt:
                            hidden(L, *nxt[:2])
                        if e == 5 and behind and L == 0:
                            message_rows(b - 1)
                        if e == 5 and ahead:
                            transposed_gates(L, b + 1, 1 - par)
                        nxt = ahead_of(b, e, par, 2)
                        if nxt:
                            high_hidden(L, *nxt[:2])
                        if e == 1 and ahead:
                            transposed_rows(L, b + 1, 1 - par)
                    act.wait_ge(w2_done, expert_no(L, b, E - 1) + (NP + 1))
                    nc.scalar.activation(YS[:, :], YB, ACT.Copy).then_inc(y_out, 1)

                blocks(act, body)
                if L == 0:
                    act.preload_act_table_set("natural_log_exp_and_others")
                    invert_first(0, 0)
                    invert_second(0, 0)
                    message_rows(NB - 1)

            experts(0)

            def sensitivity(u, s):
                act.wait_ge(square, u + 1)
                nc.scalar.activation(ring[s][:, :], ring[s][:, :], ACT.Exp, scale=-2.0,
                                     bias=minus2[:, :]).then_inc(f_ready, 1)

            def stream(g):
                for s in range(S2):
                    if not (first(g) and s == 0):
                        invert_second(g * S2 + s, s)
                    invert_first(g * S2 + (s + 1), (s + 1) % S2)
                    if not (first(g) and s == 0):
                        sensitivity(g * S2 + (s - 1), (s - 1) % S2)

            stream(0)
            with act.Fori(1, NG) as g:
                stream(g)
            for s in range(2):
                invert_second(NG * S2 + s, s)
                if s == 0:
                    invert_first(NG * S2 + 1, 1)
                sensitivity(NG * S2 + s - 1, (s - 1) % S2)
            sensitivity(NG * S2 + 1, 1)
            evacuate(1)
            experts(1)

        @block.tensor
        def _(pe):
            pe.sem_inc(prod1, S1)
            pe.sem_inc(prod_a, 1)
            pe.sem_inc(w2_done, NP)
            pe.sem_inc(prod2, 2)

            def graph_rows(L, b):
                pe.wait_ge(staged, b + (NB * L + 1))
                if not (first(b) and L == 0):
                    pe.wait_ge(mp_free, mp_no(L, b, 0))
                for k in range(K4):
                    a = AGS[:, k * P:(k + 1) * P]
                    if L == 0:
                        ins = nc.tensor.matmul(MP[:, k * P:(k + 1) * P], a, Kw[:, :], start=True, stop=True)
                    else:
                        ins = nc.tensor.transpose(MP[:, k * P:(k + 1) * P], a, ident[:, :])
                ins.then_inc(mp_ready, 1)

            def product(xslot, adj, start, stop):
                for b in range(NB):
                    ins = nc.tensor.matmul(bank[:, b, :], xs[xslot][:, :], adj[:, b * BK:(b + 1) * BK],
                                           start=start, stop=stop)
                    if stop:
                        ins.then_inc(bank_done[1], 1)
                        if b == 3:
                            early_rows(1)
                return ins

            def early_rows(L):
                if L == 0:
                    pe.wait_ge(kw_ready, 1)
                    pe.wait_ge(evac_a[0], 1)
                graph_rows(L, 0)
                if L == 0:
                    for k in range(K4):
                        ins = nc.tensor.transpose(ME[:, k * P:(k + 1) * P], AGS[:, k * P:(k + 1) * P], ident[:, :])
                    ins.then_inc(sums_ready, 1)

            def graph1(t, s, x, start=False, stop=False, cached=None):
                pe.wait_ge(tile_ready, t + 1)
                for b in range(NF):
                    src = (ring1[s][:, b * BK:(b + 1) * BK] if cached is None
                           else C[:, bass.ds(cached * N + b * BK, BK)])
                    ins = nc.tensor.matmul(bank[:, b, :], xs[x][:, :], src, start=start, stop=stop)
                    if stop:
                        ins.then_inc(bank_done[0], 1)
                pe.wait_ge(xs_ready, t + 1)
                for part, (b0, b1) in enumerate(PARTS):
                    pe.wait_ge(lo1_ready, t * 2 + (part + 1))
                    for b in range(b0, b1):
                        h = hi1[:, (b - NF) * BK:(b - NF + 1) * BK]
                        nc.tensor.matmul(bank[:, b, :], xsh[x][:, :], h, start=start, stop=False)
                        nc.tensor.matmul(bank[:, b, :], xsl[x][:, :], h, start=False, stop=False)
                        ins = nc.tensor.matmul(bank[:, b, :], xsh[x][:, :], lo1[s][:, b * BK:(b + 1) * BK],
                                               start=False, stop=stop)
                        if stop:
                            ins.then_inc(bank_done[0], 1)
                    if stop and part == 0:
                        early_rows(0)
                    if not stop:
                        ins.then_inc(prod_a if part == 0 else prod1, 1)

            graph1(0, 0, 0, start=True)
            with pe.Fori(0, NG) as g:
                for k in range(G):
                    t = 1 + k
                    graph1(g * G + t, t % S1, t % 2, cached=g if k == 0 else None)
            graph1(T - 1, (T - 1) % S1, (T - 1) % 2, stop=True)

            def row_sums():
                for b in range(1, NB):
                    for k in range(K4):
                        ins = nc.tensor.transpose(bank[:, b, k * P:(k + 1) * P],
                                                  AG[:, b * BK + k * P:b * BK + (k + 1) * P], ident[:, :])
                ins.then_inc(sums_ready, 1)

            def transpose_rows(L, b):
                pe.wait_ge(normed, n_no(L, b) + 1)
                pe.wait_ge(mp_free, mp_no(L, b, 1))
                for k in range(K4):
                    ins = nc.tensor.transpose(MP[:, k * P:(k + 1) * P], XL[:, k * P:(k + 1) * P], ident[:, :])
                ins.then_inc(mp_ready, 1)

            def logits(L, b):
                pe.wait_ge(mp_free, mp_no(L, b, 2))
                for k in range(K4):
                    ins = nc.tensor.matmul(MP[:, k * E:(k + 1) * E], xT[:, k * P:(k + 1) * P], Wrt[L][:, :],
                                           start=True, stop=True)
                ins.then_inc(mp_ready, 1)

            def transpose_gates(L, b):
                pe.wait_ge(gates_ready, b + (NB * L + 1))
                pe.wait_ge(mp_free, mp_no(L, b, 3))
                for k in range(K4):
                    ins = nc.tensor.transpose(MP[0:2 * E, k * P:(k + 1) * P], wcat[:, k, :], ident[:, :])
                ins.then_inc(mp_ready, 1)

            def transpose_output(L, b):
                pe.wait_ge(y_out, b + (NB * L + 1))
                if not (first(b) and L == 0):
                    pe.wait_ge(me_free, me_no(L, b, 0))
                for k in range(K4):
                    ins = nc.tensor.transpose(ME[:, k * P:(k + 1) * P], YS[:, k * P:(k + 1) * P], ident[:, :])
                ins.then_inc(me_ready, 1)

            def transpose_messages(b):
                pe.wait_ge(e_normed, b + 1)
                pe.wait_ge(me_free, me_no(0, b, 1))
                for k in range(K4):
                    ins = nc.tensor.transpose(ME[:, k * P:(k + 1) * P], XLe[:, k * P:(k + 1) * P], ident[:, :])
                ins.then_inc(me_ready, 1)

            def messages(b):
                pe.wait_ge(me_free, me_no(0, b, 2))
                for k in range(K4):
                    ins = nc.tensor.matmul(ME[:, k * P:(k + 1) * P], xTe[:, k * P:(k + 1) * P], Wm[:, :],
                                           start=True, stop=True)
                ins.then_inc(me_ready, 1)

            def up(L, b, e, par):
                n = expert_no(L, b, e)
                s = e % 2
                if e == 0:
                    pe.wait_ge(xt_ready, b + (NB * L + 1))
                for c in range(HC):
                    pe.wait_ge(acted, n * 2 + (c + 1))
                    w = slice((e * HC + c) * P, (e * HC + c + 1) * P)
                    nc.tensor.matmul(HB[s][:, c, :], W1h[L][:, w], XTh[par][:, :], start=True, stop=False)
                    nc.tensor.matmul(HB[s][:, c, :], W1h[L][:, w], XTl[par][:, :], start=False, stop=False)
                    nc.tensor.matmul(HB[s][:, c, :], W1l[L][:, w], XTh[par][:, :], start=False,
                                     stop=True).then_inc(hid_ready, 1)

            def gate(L, b, e, par):
                if e == 0:
                    pe.wait_ge(mp_free, mp_no(L, b, 3) + 1)
                pe.wait_ge(gated, expert_no(L, b, e) + 2)
                nc.tensor.matmul(GB, sel[:, e * P:(e + 1) * P], wT[par][:, :], start=True,
                                 stop=True).then_inc(gb_ready, 1)

            def output_bias(L, b, par):
                if not (first(b) and L == 0):
                    pe.wait_ge(y_out, b + NB * L)
                nc.tensor.matmul(YB, b2h[L][:, :], wT[par][:, :], start=True, stop=False)
                nc.tensor.matmul(YB, b2l[L][:, :], wT[par][:, :], start=False, stop=False)

            def down(L, b, e):
                n = expert_no(L, b, e)
                pe.wait_ge(hi_ready, n + 1)
                for c in range(HC):
                    w = slice((e * HC + c) * D, (e * HC + c + 1) * D)
                    nc.tensor.matmul(YB, W2h[L][:, w], hhi[e % 2][:, c, :], start=False, stop=False)
                    nc.tensor.matmul(YB, W2l[L][:, w], hhi[e % 2][:, c, :], start=False, stop=False)
                for c in range(HC):
                    pe.wait_ge(lo_ready, n * 2 + (c + 1))
                    w = slice((e * HC + c) * D, (e * HC + c + 1) * D)
                    ins = nc.tensor.matmul(YB, W2h[L][:, w], hlo[e % NP][:, c, :],
                                           start=False, stop=(e == E - 1 and c == HC - 1))
                ins.then_inc(w2_done, 1)

            def experts(L):
                transpose_rows(L, 0)
                logits(L, 0)
                pe.wait_ge(evac_a[L], 3)
                pe.wait_ge(evac_v[L], 4)
                if L == 0:
                    pe.wait_ge(scl_ready, 1)
                    row_sums()
                    transpose_gates(L, 0)
                    pe.wait_ge(scl_ready, 2)
                pe.wait_ge(split1, 3 * L + 3)
                up(L, 0, 0, 0)
                if L == 1:
                    transpose_gates(L, 0)
                up(L, 0, 1, 0)
                gate(L, 0, 0, 0)
                up(L, 0, 2, 0)
                gate(L, 0, 1, 0)
                pe.wait_ge(split2, 3 * L + 3)

                def body(b, par):
                    ahead, behind = not last(b), not first(b)
                    for e in range(E):
                        if e == 0 and ahead:
                            graph_rows(L, b + 1)
                        nxt = ahead_of(b, e, par, 3)
                        if nxt:
                            up(L, *nxt)
                        nxt = ahead_of(b, e, par, 2)
                        if nxt:
                            gate(L, *nxt)
                        if e == 0:
                            output_bias(L, b, par)
                        if e == 5 and ahead:
                            transpose_gates(L, b + 1)
                        down(L, b, e)
                        if e == 1 and behind:
                            transpose_output(L, b - 1)
                        if e == 1 and ahead:
                            transpose_rows(L, b + 1)
                        if e == 2 and ahead:
                            logits(L, b + 1)
                        if e == 4 and behind and L == 0:
                            transpose_messages(b - 1)
                        if e == 6 and behind and L == 0:
                            messages(b - 1)

                blocks(pe, body)
                transpose_output(L, NB - 1)
                if L == 0:
                    transpose_messages(NB - 1)
                    messages(NB - 1)

            experts(0)
            pe.wait_ge(me_free, NB * M_END[0])
            pe.wait_ge(y_out, NB)
            pe.wait_ge(c_ready, 2 * NG)

            def graph2_cached(g, banks, start=False):
                pe.wait_ge(msg_staged, g * G + 1)
                for b in banks:
                    ins = nc.tensor.matmul(bank[:, b, :], xs[0][:, :], C[:, bass.ds(g * N + b * BK, BK)],
                                           start=start, stop=False)
                return ins

            def graph2_streamed(k, u, s, count=1):
                pe.wait_ge(msg_staged, k + 1)
                pe.wait_ge(f_ready, u + 1)
                product((1 + s) % 3, ring[s], False, False).then_inc(prod2, count)

            def group(g, start=False):
                graph2_cached(g, range(NB if start else NB // 2), start)
                for s in range(S2):
                    graph2_streamed(g * G + (1 + s), g * S2 + s, s, 2 if start and s == 0 else 1)
                    if s == 0 and not start:
                        graph2_cached(g, range(NB // 2, NB)).then_inc(prod2, 1)

            group(0, start=True)
            with pe.Fori(1, NG) as g:
                group(g)
            for s in range(2):
                pe.wait_ge(msg_staged, T - 1 + s)
                pe.wait_ge(f_ready, NG * S2 + s + 1)
                ins = product(s, ring[s], False, s == 1)
                if s == 0:
                    ins.then_inc(prod2, 1)
            experts(1)


def kernel(x, adj, L0_gnn_kernel, L0_gnn_bias, L0_gnn_beta, L0_ffn_gamma, L0_ffn_beta, L0_ffn_Wr, L0_ffn_br,
           L0_ffn_W1, L0_ffn_b1, L0_ffn_W2, L0_ffn_b2, L1_gnn_W, L1_gnn_B, L1_ffn_Wg, L1_ffn_bg, L1_ffn_bias,
           L1_ffn_W1, L1_ffn_b1, L1_ffn_W2, L1_ffn_b2):
    import numpy as np
    import concourse.bacc as bacc
    from concourse import mybir as mb
    from concourse.bass_utils import run_bass_kernel_spmd

    N, D = np.shape(x)
    P = 128

    def rows(a):
        return np.asarray(a).reshape(N // P, P, D).transpose(1, 0, 2).reshape(P, -1)

    def up(w):
        return np.asarray(w).transpose(1, 0, 2).reshape(D, -1)

    def chunks(w):
        w = np.asarray(w)
        return w.reshape(w.shape[0], w.shape[1] // P, P, -1).transpose(2, 0, 1, 3).reshape(P, -1)

    ins = {
        "x_t": rows(x), "adj_t": np.asarray(adj).T, "kern0": L0_gnn_kernel, "bias0": L0_gnn_bias,
        "beta_t": np.asarray(L0_gnn_beta).reshape(N // P, P).T,
        "gamma": np.asarray(L0_ffn_gamma).reshape(D, 1), "beta_ln": np.asarray(L0_ffn_beta).reshape(D, 1),
        "wr": L0_ffn_Wr, "br": L0_ffn_br, "w1a": up(L0_ffn_W1), "b1a": chunks(L0_ffn_b1),
        "w2a": chunks(L0_ffn_W2), "b2a": L0_ffn_b2, "wm": L1_gnn_W, "bm": L1_gnn_B,
        "wg": L1_ffn_Wg, "bg": L1_ffn_bg, "gate_bias": L1_ffn_bias, "w1b": up(L1_ffn_W1),
        "b1b": chunks(L1_ffn_b1), "w2b": chunks(L1_ffn_W2), "b2b": L1_ffn_b2,
    }
    nc = bacc.Bacc("TRN2", target_bir_lowering=False, num_devices=1)
    arrays, args = {}, []
    for name, a in ins.items():
        a = np.ascontiguousarray(a)
        arrays[f"in_{name}"] = a
        args.append(nc.dram_tensor(f"in_{name}", a.shape, mb.dt.from_np(a.dtype), kind="ExternalInput").ap())
    args.append(nc.dram_tensor("out_x", (P, N), mb.dt.float32, kind="ExternalOutput").ap())
    gnn_moe_two_layers(nc, *args)
    r = run_bass_kernel_spmd(nc, [arrays], core_ids=[0])
    got = r.results[0]["out_x"]
    return got.reshape(P, N // P, D).transpose(1, 0, 2).reshape(N, D)
```
